# Optimizing a Trainium2 kernel written in Bass

```python
import numpy as np
import jax
import jax.numpy as jnp

def _softmax(x, axis=-1):
    return jax.nn.softmax(x, axis=axis)

def _gelu(x):
    return jax.nn.gelu(x, approximate=True)

def _silu(x):
    return jax.nn.silu(x)

def _sigmoid(x):
    return jax.nn.sigmoid(x)

def _layernorm(x, axis=-1, eps=1e-05):
    m = jnp.mean(x, axis=axis, keepdims=True)
    v = jnp.var(x, axis=axis, keepdims=True)
    return (x - m) / jnp.sqrt(v + eps)

def _scatter_add(tgt, idx, src, axis=0):
    return tgt.at[idx].add(src)

def _segment_sum(src, seg, n):
    return jax.ops.segment_sum(src, seg, n)
kernel_name = 'mk_decoder_preln_d1_seqx_r4_f80cf7'

def setup_inputs(seed: int=0):
    np.random.seed(seed)
    _w = jnp.asarray

    def _rec_inputs():
        import jax
        import jax.numpy as jnp
        _rk = jax.random.key(seed)
        x = -0.0002928 + 1 * jax.random.normal(jax.random.fold_in(_rk, 1), (4, 512, 256), jnp.float32)
        _lenS = 512 - jax.random.randint(jax.random.fold_in(_rk, 7), (4,), 0, max(1, 512 // 4) + 1, jnp.int32)
        _lenS2 = 512 - jax.random.randint(jax.random.fold_in(_rk, 8), (4,), 0, max(1, 512 // 4) + 1, jnp.int32)
        _ctx_1024P = jax.random.normal(jax.random.fold_in(_rk, 11), (4, 16, 256), jnp.float32)
        _ctx_1024c = jax.random.dirichlet(jax.random.fold_in(_rk, 511), 0.3 * jnp.ones((16,), jnp.float32), (4, 512))
        _ctx_1024t = jnp.einsum('bsk,bkd->bsd', _ctx_1024c, _ctx_1024P)
        _ctx_1024t = _ctx_1024t * jax.lax.rsqrt(jnp.mean(jnp.square(_ctx_1024t)) + 1e-12) * 0.953939
        ctx_1024 = -1.39393e-06 + 0.999914 * (_ctx_1024t + 0.3 * jax.random.normal(jax.random.fold_in(_rk, 611), (4, 512, 256), jnp.float32))
        return (x, ctx_1024)
    x, ctx_1024 = _rec_inputs()

    def _L0_attn_setup():
        import jax, jax.numpy as jnp
        import numpy as np
        B, N, D = (4, 1024, 256)
        H, DH = (16, 64)
        W = 64

        def _sliding_window_attn(q, k, v):
            BH, n, dh = q.shape
            nb = n // W
            qb = q.reshape(BH, nb, W, dh)
            pad = jnp.zeros((BH, W, dh), q.dtype)
            kp = jnp.concatenate([pad, k], axis=1).reshape(BH, nb + 1, W, dh)
            vp = jnp.concatenate([pad, v], axis=1).reshape(BH, nb + 1, W, dh)
            kw = jnp.concatenate([kp[:, :-1], kp[:, 1:]], axis=2)
            vw = jnp.concatenate([vp[:, :-1], vp[:, 1:]], axis=2)
            scores = jnp.einsum('bnqd,bnkd->bnqk', qb, kw)
            blk = jnp.arange(nb)[:, None, None]
            ii = jnp.arange(W)[None, :, None]
            jj = jnp.arange(2 * W)[None, None, :]
            mask = (jj - W <= ii) & (jj >= ii + 1) & (blk * W + jj - W >= 0)
            neg = -jnp.finfo(scores.dtype).max
            scores = jnp.where(mask[None], scores, neg)
            attn = jax.nn.softmax(scores, axis=-1)
            out = jnp.einsum('bnqk,bnkd->bnqd', attn, vw)
            return out.reshape(BH, n, dh)
        key = jax.random.key(seed)
        k1, k2, k3 = jax.random.split(key, 3)
        x = jax.random.normal(k1, (B, N, D), dtype=jnp.float32)
        w_qkv = jax.random.normal(k2, (D, 3 * H * DH), dtype=jnp.float32) * D ** (-0.5)
        w_out = jax.random.normal(k3, (H * DH, D), dtype=jnp.float32) * (H * DH) ** (-0.5)
        return {'x': x, 'w_qkv': w_qkv, 'w_out': w_out}
    _L0_attn_all = _L0_attn_setup()
    _L0_attn_in = {k: v for k, v in _L0_attn_all.items() if k in ('w_qkv', 'w_out')}
    del _L0_attn_all

    def _L0_xattn_setup():
        import jax, jax.numpy as jnp
        import numpy as np
        NUM_HEADS = 16
        key = jax.random.key(seed)
        kq, kk, kv = jax.random.split(key, 3)
        b, s, h = (1, 1024, 256)
        q = jax.random.normal(kq, (b, s, h), dtype=jnp.float32)
        k = jax.random.normal(kk, (b, s, h), dtype=jnp.float32)
        v = jax.random.normal(kv, (b, s, h), dtype=jnp.float32)
        return {'q': q, 'k': k, 'v': v}
    _L0_xattn_all = _L0_xattn_setup()
    _L0_xattn_in = {k: v for k, v in _L0_xattn_all.items() if k in ()}
    del _L0_xattn_all

    def _L0_ffn_setup():
        import jax, jax.numpy as jnp
        import numpy as np
        D_MODEL = 256
        HIDDEN = 512
        N_EXPERTS = 8
        TOP_K = 2
        BATCH = 2
        SEQ = 512
        key = jax.random.key(seed)
        ks = jax.random.split(key, 9)
        s = 0.02
        return {'x': jax.random.normal(ks[0], (BATCH, SEQ, D_MODEL), dtype=jnp.float32), 'w_router': jax.random.normal(ks[1], (D_MODEL, N_EXPERTS), dtype=jnp.float32) * s, 'w1': jax.random.normal(ks[2], (N_EXPERTS, D_MODEL, HIDDEN), dtype=jnp.float32) * s, 'w3': jax.random.normal(ks[3], (N_EXPERTS, D_MODEL, HIDDEN), dtype=jnp.float32) * s, 'w2': jax.random.normal(ks[4], (N_EXPERTS, HIDDEN, D_MODEL), dtype=jnp.float32) * s, 'sw1': jax.random.normal(ks[5], (D_MODEL, HIDDEN), dtype=jnp.float32) * s, 'sw3': jax.random.normal(ks[6], (D_MODEL, HIDDEN), dtype=jnp.float32) * s, 'sw2': jax.random.normal(ks[7], (HIDDEN, D_MODEL), dtype=jnp.float32) * s}
    _L0_ffn_all = _L0_ffn_setup()
    _L0_ffn_in = {k: v for k, v in _L0_ffn_all.items() if k in ('w_router', 'w1', 'w3', 'w2', 'sw1', 'sw3', 'sw2')}
    del _L0_ffn_all
    return {'x': x, 'ctx_1024': ctx_1024, 'L0_attn_w_qkv': _L0_attn_in['w_qkv'], 'L0_attn_w_out': _L0_attn_in['w_out'], 'L0_ffn_w_router': _L0_ffn_in['w_router'], 'L0_ffn_w1': _L0_ffn_in['w1'], 'L0_ffn_w3': _L0_ffn_in['w3'], 'L0_ffn_w2': _L0_ffn_in['w2'], 'L0_ffn_sw1': _L0_ffn_in['sw1'], 'L0_ffn_sw3': _L0_ffn_in['sw3'], 'L0_ffn_sw2': _L0_ffn_in['sw2']}

def reference(x, ctx_1024, L0_attn_w_qkv, L0_attn_w_out, L0_ffn_w_router, L0_ffn_w1, L0_ffn_w3, L0_ffn_w2, L0_ffn_sw1, L0_ffn_sw3, L0_ffn_sw2):
    import jax
    import jax.numpy as jnp

    def _L0_attn_ref(x, w_qkv, w_out):
        import jax, jax.numpy as jnp
        import numpy as np
        B, N, D = (4, 1024, 256)
        H, DH = (16, 64)
        W = 64

        def _sliding_window_attn(q, k, v):
            BH, n, dh = q.shape
            nb = n // W
            qb = q.reshape(BH, nb, W, dh)
            pad = jnp.zeros((BH, W, dh), q.dtype)
            kp = jnp.concatenate([pad, k], axis=1).reshape(BH, nb + 1, W, dh)
            vp = jnp.concatenate([pad, v], axis=1).reshape(BH, nb + 1, W, dh)
            kw = jnp.concatenate([kp[:, :-1], kp[:, 1:]], axis=2)
            vw = jnp.concatenate([vp[:, :-1], vp[:, 1:]], axis=2)
            scores = jnp.einsum('bnqd,bnkd->bnqk', qb, kw)
            blk = jnp.arange(nb)[:, None, None]
            ii = jnp.arange(W)[None, :, None]
            jj = jnp.arange(2 * W)[None, None, :]
            mask = (jj - W <= ii) & (jj >= ii + 1) & (blk * W + jj - W >= 0)
            neg = -jnp.finfo(scores.dtype).max
            scores = jnp.where(mask[None], scores, neg)
            attn = jax.nn.softmax(scores, axis=-1)
            out = jnp.einsum('bnqk,bnkd->bnqd', attn, vw)
            return out.reshape(BH, n, dh)
        b, n, d = x.shape
        qkv = x @ w_qkv
        q, k, v = jnp.split(qkv, 3, axis=-1)

        def to_heads(t):
            return t.reshape(b, n, H, DH).transpose(0, 2, 1, 3).reshape(b * H, n, DH)
        q, k, v = map(to_heads, (q, k, v))
        q = q * DH ** (-0.5)
        out = _sliding_window_attn(q, k, v)
        out = out.reshape(b, H, n, DH).transpose(0, 2, 1, 3).reshape(b, n, H * DH)
        return out @ w_out

    def _L0_xattn_ref(q, k, v):
        import jax, jax.numpy as jnp
        import numpy as np
        NUM_HEADS = 16
        b, s, hd = q.shape
        n = NUM_HEADS
        d = hd // n
        qh = q.reshape(b, s, n, d)
        kh = k.reshape(b, s, n, d)
        vh = v.reshape(b, s, n, d)
        scale = 1.0 / jnp.sqrt(jnp.float32(d))
        scores = jnp.einsum('bqnd,bknd->bnqk', qh, kh) * scale
        probs = jax.nn.softmax(scores, axis=-1)
        out = jnp.einsum('bnqk,bknd->bqnd', probs, vh)
        return out.reshape(b, s, hd)

    def _L0_ffn_ref(x, w_router, w1, w3, w2, sw1, sw3, sw2):
        import jax, jax.numpy as jnp
        import numpy as np
        D_MODEL = 256
        HIDDEN = 512
        N_EXPERTS = 8
        TOP_K = 2
        BATCH = 2
        SEQ = 512
        b, s, d = x.shape
        xf = x.reshape(b * s, d)
        probs = jax.nn.softmax(xf @ w_router, axis=-1)
        top_vals, top_idx = jax.lax.top_k(probs, TOP_K)
        gates = top_vals / jnp.sum(top_vals, axis=-1, keepdims=True)
        onehot = jax.nn.one_hot(top_idx, N_EXPERTS, dtype=xf.dtype)
        cw = jnp.einsum('tk,tke->te', gates, onehot)
        h1 = jnp.einsum('td,edh->eth', xf, w1)
        h3 = jnp.einsum('td,edh->eth', xf, w3)
        y = jnp.einsum('eth,ehd->etd', jax.nn.silu(h1) * h3, w2)
        out = jnp.einsum('etd,te->td', y, cw)
        out = out + jax.nn.silu(xf @ sw1) * (xf @ sw3) @ sw2
        return out.reshape(b, s, d)
    x = x + _L0_attn_ref(_layernorm(x, axis=-1), L0_attn_w_qkv, L0_attn_w_out)
    x = x + _L0_xattn_ref(_layernorm(x, axis=-1), ctx_1024, ctx_1024)
    x = x + _L0_ffn_ref(_layernorm(x, axis=-1), L0_ffn_w_router, L0_ffn_w1, L0_ffn_w3, L0_ffn_w2, L0_ffn_sw1, L0_ffn_sw3, L0_ffn_sw2)
    return x

_drawn_inputs = setup_inputs


def setup_inputs(seed=0):
    import zlib

    import numpy as np

    out = dict(_drawn_inputs(seed))
    spreads = {}
    factors = {'L0_ffn_w_router': 5.103,
     'L0_ffn_w1': 4.463,
     'L0_ffn_w3': 4.413,
     'L0_ffn_w2': 4.407,
     'L0_ffn_sw1': 3.186,
     'L0_ffn_sw3': 3.132,
     'L0_ffn_sw2': 3.154}
    for name, (base, spread) in spreads.items():
        noise = np.random.default_rng([zlib.crc32(name.encode()), seed]).standard_normal(out[name].shape)
        drawn = base * np.exp(spread * noise) if base else spread * noise
        out[name] = jnp.asarray(drawn.astype(out[name].dtype))
    for name, factor in factors.items():
        out[name] = (out[name] * factor).astype(out[name].dtype)
    return out
```

```python
from contextlib import ExitStack

import concourse.bass as bass
import concourse.mybir as mybir
from concourse.alu_op_type import AluOpType as ALU

F32 = mybir.dt.float32
BF16 = mybir.dt.bfloat16
U32 = mybir.dt.uint32
ACT = mybir.ActivationFunctionType
AXX = mybir.AxisListType.X

P = 128
B, S, D = 4, 512, 256
T = B * S
NT = T // P
QT = S // P
DC = D // P
H = 16
DH = 64
HP = H * DH // P
W = 64
KW = W + P
XD = D // H
XS = 6 * XD
HG = 4
NG = H // HG
NE = 8
F = 512
FC = F // P
EPS = 1e-5
MASKED = -3.0e38
RING = (4, 5, 7)


def decoder_layer(nc, x, ctx, w_qkv, w_out, w_router, w1, w3, w2, sw1, sw3, sw2, out):
    with ExitStack() as es:
        def sb(name, shape, dt=F32):
            return es.enter_context(nc.sbuf_tensor(name, shape, dt))

        def sem(name):
            return es.enter_context(nc.semaphore(name))

        ps = es.enter_context(nc.psum_tensor("ps", [P, 8, 512], F32))

        xs = sb("xs", [P, NT, D])
        xn = sb("xn", [P, NT, D])
        xnT = sb("xnT", [P, DC, T])
        cs = sb("cs", [P, NT, D])
        stats = sb("stats", [P, NT, 6])
        mv = sb("mv", [P, NT, 2])
        std = sb("std", [P, NT])
        rstd = sb("rstd", [P, NT])
        ident = sb("ident", [P, P])
        ident_b = sb("ident_b", [P, P], BF16)
        mask = sb("mask", [P, 2, KW], BF16)

        wqkv = sb("wqkv", [P, DC, 3, P])
        wo = sb("wo", [P, D])
        qa = sb("qa", [P, 2, S])
        qb = sb("qb", [P, 2, S])
        kt = sb("kt", [P, 2, W + S])
        vv = sb("vv", [P, 2, QT, P])
        pr = sb("pr", [P, 2, QT, 2, 2 * P])
        prT = sb("prT", [P, 2, QT, KW])
        oT = sb("oT", [P, S])
        nmax = sb("nmax", [P, 2, 2 * QT])
        rsum = sb("rsum", [P, 2, 2 * QT])
        rinv = sb("rinv", [P, 2, 2 * QT])

        part = sb("part", [P, 2, 3, S], BF16)
        rest = sb("rest", [P, 2, S])
        qp = sb("qp", [XS + 2, H, S], BF16)
        kp = sb("kp", [XS + 2, H, S], BF16)
        vp = sb("vp", [P, QT, H, 32])
        ex = sb("ex", [P, 2, HG, S])
        xnm = sb("xnm", [P, 2, HG, QT])
        xm2 = sb("xm2", [P, 2, 2, HG, QT], BF16)
        xmT = sb("xmT", [2 * HG, S], BF16)
        xoT = sb("xoT", [P, S])
        xr = sb("xr", [P, QT, HG])
        xo = sb("xo", [P, QT, HG, XD])

        wr = sb("wr", [P, DC, NE])
        wa = sb("wa", [P, 2, DC, F])
        wb = sb("wb", [P, 2, DC, F])
        wc = cs[:, 0:2 * FC, :].rearrange("p (e c) d -> p e c d", e=2)
        gt = prT[:, :, :, :].rearrange("p h t k -> p (h t k)")[:, 0:2 * S].rearrange("p (i s) -> p i s", i=2)
        ht = pr[:, :, :, :, :].rearrange("p a b c d -> p (a b c d)").rearrange("p (i m s) -> p i m s", i=2, m=FC)
        lg = sb("lg", [P, NT, NE])
        lmax = sb("lmax", [P, NT])
        pe8 = sb("pe8", [P, NT, NE])
        top = sb("top", [P, NT, 8])
        tix = sb("tix", [P, NT, 8], U32)
        tixf = sb("tixf", [P, NT, 2])
        gsum = sb("gsum", [P, NT])
        gate = sb("gate", [P, NT, 2])
        iota8 = sb("iota8", [P, NE])
        hot = sb("hot", [P, 2, NT, NE])
        cw = sb("cw", [P, NT, NE])

        scr_q = nc.dram_tensor("scr_q", (H, 3, XD, T), BF16, kind="Internal").ap()
        scr_k = nc.dram_tensor("scr_k", (H, 3, XD, T), BF16, kind="Internal").ap()

        x_loaded = [sem(f"x_loaded{b}") for b in range(B)]
        c_loaded = sem("c_loaded")
        stats_ready, mv_ready, var_ready, std_ready = sem("stats_ready"), sem("mv_ready"), sem("var_ready"), sem("std_ready")
        rstd_ready, xn_ready = sem("rstd_ready"), sem("xn_ready")
        turned, xnT_ready = sem("turned"), sem("xnT_ready")
        zeroed, consts_ready = sem("zeroed"), sem("consts_ready")
        hi_ready, rest1_ready, mid_ready, parts_ready = sem("hi_ready"), sem("rest1_ready"), sem("mid_ready"), sem("parts_ready")
        parts_stored = [sem("parts_stored0"), sem("parts_stored1")]

        wqkv_loaded, wo_loaded = sem("wqkv_loaded"), sem("wo_loaded")
        q_filled, k_filled, v_filled = sem("q_filled"), sem("k_filled"), sem("v_filled")
        q_ready, k_ready, v_ready = sem("q_ready"), sem("k_ready"), sem("v_ready")
        scores_filled, max_ready, exp_done = sem("scores_filled"), sem("max_ready"), sem("exp_done")
        rinv_ready, probs_ready = sem("rinv_ready"), sem("probs_ready")
        prT_filled, prT_ready = sem("prT_filled"), sem("prT_ready")
        oT_filled, oT_ready, y_filled = sem("oT_filled"), sem("oT_ready"), sem("y_filled")
        x1_ready = sem("x1_ready")

        split_loaded = [sem(f"split_loaded{g}") for g in range(NG)]
        vp_ready = sem("vp_ready")
        xs_filled = sem("xs_filled")
        nmax_ready, part1_ready, m2_ready = sem("nmax_ready"), sem("part1_ready"), sem("m2_ready")
        m2T_filled, m2T_ready, m_loaded = sem("m2T_filled"), sem("m2T_ready"), sem("m_loaded")
        st_filled, ex_ready, pv_done = sem("st_filled"), sem("ex_ready"), sem("pv_done")
        xoT_ready, xoN_filled, xr_ready, xo_ready, x2_ready = sem("xoT_ready"), sem("xoN_filled"), sem("xr_ready"), sem("xo_ready"), sem("x2_ready")

        wr_loaded, logits_filled, route = sem("wr_loaded"), sem("logits_filled"), sem("route")
        e_ready, exp_e_ready = sem("e_ready"), sem("exp_e_ready")
        expert_loaded = [sem("expert_loaded0"), sem("expert_loaded1")]
        h_filled, silu_ready, h_ready = sem("h_filled"), sem("silu_ready"), sem("h_ready")
        e_filled, e_added, x3_stored = sem("e_filled"), sem("e_added"), sem("x3_stored")

        x_in = x.rearrange("b (t p) d -> b p t d", p=P)
        c_in = ctx.rearrange("b (t p) d -> p (b t) d", p=P)
        y_out = out.rearrange("b (t p) d -> b p t d", p=P)
        wqkv_in = w_qkv.rearrange("(c p) (s h n) -> c p s h n", p=P, s=3, h=HP)
        wo_in = w_out.rearrange("(h p) n -> h p n", p=P)

        w1_in, w3_in = (w.rearrange("e (c p) f -> e p c f", p=P) for w in (w1, w3))
        w2_in = w2.rearrange("e (c p) d -> e p c d", p=P)
        sw1_in, sw3_in, sw2_in = (w.rearrange("(c p) f -> p c f", p=P) for w in (sw1, sw3, sw2))

        def ln_vector(dve, n, x_waits):
            for t in range(NT):
                for s, v in x_waits(t):
                    dve.wait_ge(s, v)
                nc.vector.bn_stats(stats[:, t, :], xs[:, t, :]).then_inc(stats_ready, 1)
            dve.wait_ge(stats_ready, NT * (n + 1))
            for t in range(NT):
                nc.vector.bn_aggr(mv[:, t, :], stats[:, t, :]).then_inc(mv_ready, 1)
            dve.wait_ge(mv_ready, NT * (n + 1))
            nc.vector.tensor_scalar(rstd[:, :], mv[:, :, 1], EPS, None, ALU.add).then_inc(var_ready, 1)
            dve.wait_ge(std_ready, n + 1)
            nc.vector.reciprocal(rstd[:, :], std[:, :]).then_inc(rstd_ready, 1)
            dve.wait_ge(rstd_ready, n + 1)
            for t in range(NT):
                nc.vector.tensor_scalar(xn[:, t, :], xs[:, t, :], mv[:, t, 0:1], rstd[:, t:t + 1],
                                        ALU.subtract, ALU.mult).then_inc(xn_ready, 1)

        def ln_scalar(act, n):
            act.wait_ge(var_ready, n + 1)
            nc.scalar.activation(std[:, :], rstd[:, :], ACT.Sqrt).then_inc(std_ready, 1)

        def turn(pe, src, b, c, bank, done):
            for t in range(QT):
                mm = nc.tensor.transpose(ps[:, bank, t * P:(t + 1) * P], src[:, QT * b + t, c * P:(c + 1) * P], ident[:])
            mm.then_inc(done, 1)

        order = []
        for b in range(B):
            if b >= 1:
                order += [("pT", b - 1, t) for t in range(QT)] + [("y", b - 1, i) for i in range(2)]
            order += [(s, (b + 1) % B, 0) for s in "qkv"]
        order += [("pT", B - 1, t) for t in range(QT)] + [("y", B - 1, i) for i in range(2)]
        bank_of = {use: RING[n % 3] for n, use in enumerate(order)}

        def bank_left(use, hp, last):
            at = order.index(use)
            if last and order[at - 3][0] in "qkv" and order[at - 3][1] == 0:
                at -= 3
            if at < 3:
                return [(x1_ready, 1 + 2 * B * hp), (v_ready, B * hp + 1)]
            name, b, i = order[at - 3]
            n = (hp + 1) * B if name in "qkv" and b == 0 else hp * B + b
            return {"q": [(q_ready, 2 * n + 2)], "k": [(k_ready, n + 1)], "v": [(v_ready, n + 1)],
                    "pT": [(prT_ready, 7 * n + 2 * i + 1)], "y": [(x1_ready, 2 * n + i + 2)]}[name]

        block = es.enter_context(nc.Block())

        @block.sync
        def _(sp):
            for b in range(B):
                sp.dma_start(xs[:, QT * b:QT * (b + 1), :], x_in[b]).then_inc(x_loaded[b], 16)
            for c in range(DC):
                sp.dma_start(wqkv[:, c, :, :], wqkv_in[c, :, :, 0, :]).then_inc(wqkv_loaded, 16)
            sp.dma_start(wo[:, :], wo_in[0]).then_inc(wo_loaded, 16)
            sp.dma_start(cs[:, :, :], c_in).then_inc(c_loaded, 16)

            def store_parts(scr, n0):
                for n in range(B * DC):
                    b, c = n // DC, n % DC
                    sp.wait_ge(parts_ready, n0 + n + 1)
                    for i in range(3):
                        sp.dma_start(scr[c * 8:(c + 1) * 8, i, :, b * S:(b + 1) * S], part[:, n % 2, i, :]).then_inc(parts_stored[n % 2], 16)

            store_parts(scr_k, 0)

            with sp.Fori(0, HP - 1) as hp:
                sp.wait_ge(v_filled, hp * B + B)
                for c in range(DC):
                    sp.dma_start(wqkv[:, c, :, :], wqkv_in[c, :, :, hp + 1, :]).then_inc(wqkv_loaded, 16)
                sp.wait_ge(y_filled, hp * 2 * B + 2 * B)
                sp.dma_start(wo[:, :], wo_in[hp + 1]).then_inc(wo_loaded, 16)

            store_parts(scr_q, B * DC)
            for i in range(2):
                sp.wait_ge(parts_stored[i], 16 * 3 * B * DC)

            def load_split(b, g):
                hs = slice(HG * g, HG * (g + 1))
                ts = bass.ds(b * S, S)
                for rows, parts, scr, dst in ((0, (0, 1, 2), scr_q, qp), (3 * XD, (0, 1), scr_q, qp), (5 * XD, (0,), scr_q, qp)):
                    n = XD * len(parts)
                    src = scr.rearrange("h i d t -> (i d) h t")[0:n, hs, ts]
                    sp.dma_start(dst[rows:rows + n, hs, :], src).then_inc(split_loaded[g], 16)
                for seg, i in enumerate((0, 0, 0, 1, 1, 2)):
                    src = scr_k[hs, i, :, ts].rearrange("h d t -> d h t")
                    sp.dma_start(kp[XD * seg:XD * (seg + 1), hs, :], src).then_inc(split_loaded[g], 16)

            def load_max(n, g):
                sp.wait_ge(m2T_ready, n + 1)
                for i in range(2):
                    sp.dma_start(qp[XS + i:XS + i + 1, HG * g:HG * (g + 1), :], xmT[HG * i:HG * (i + 1), :]).then_inc(m_loaded, 16)

            for g in range(NG):
                load_split(0, g)
            load_max(0, 0)
            with sp.Fori(0, B - 1) as b:
                for g in range(NG):
                    n = b * NG + g
                    load_max(n + 1, (g + 1) % NG)
                    sp.wait_ge(st_filled, 16 * (n + 1))
                    load_split(b + 1, g)
            for g in range(NG - 1):
                load_max((B - 1) * NG + g + 1, g + 1)

            def load_expert(par, s1, s3, s2):
                for dst, src in ((wa, s1), (wb, s3), (wc, s2)):
                    sp.dma_start(dst[:, par, :, :], src).then_inc(expert_loaded[par], 16)

            sp.dma_start(wr[:, :, :], w_router.rearrange("(c p) e -> p c e", p=P)).then_inc(wr_loaded, 16)
            sp.wait_ge(vp_ready, B * QT)
            for e in range(2):
                load_expert(e, w1_in[e], w3_in[e], w2_in[e])
            with sp.Fori(0, NE // 2 - 1) as i:
                for j in range(2):
                    sp.wait_ge(e_filled, 2 * B * (2 * i + j + 1))
                    load_expert(j, *(w[2 * i + j + 2] for w in (w1_in, w3_in, w2_in)))
            sp.wait_ge(e_filled, 2 * B * (NE - 1))
            load_expert(0, sw1_in, sw3_in, sw2_in)
            for b in range(B):
                sp.wait_ge(e_added, 4 * (B * NE + b + 1))
                sp.dma_start(y_out[b], xs[:, QT * b:QT * (b + 1), :]).then_inc(x3_stored, 16)
            sp.wait_ge(x3_stored, 16 * B)

        @block.gpsimd
        def _(pool):
            nc.gpsimd.memset(ident[:], 0.0).then_inc(zeroed, 1)
            nc.gpsimd.memset(mask[:], 0.0).then_inc(zeroed, 1)
            nc.gpsimd.iota(iota8[:], [[1, NE]], base=0, channel_multiplier=0,
                           allow_small_or_imprecise_dtypes=True).then_inc(consts_ready, 1)
            nc.gpsimd.memset(qa[:], 0.0).then_inc(consts_ready, 1)
            nc.gpsimd.memset(qb[:], 0.0).then_inc(consts_ready, 1)
            nc.gpsimd.memset(kt[:], 0.0).then_inc(consts_ready, 1)
            nc.gpsimd.memset(pr[:, :, :, :, 0:W], 0.0).then_inc(consts_ready, 1)
            nc.gpsimd.memset(vp[:], 0.0).then_inc(zeroed, 1)
            pool.wait_ge(zeroed, 3)
            nc.gpsimd.memset(kp[XS:XS + 2, :, :], 1.0).then_inc(consts_ready, 1)
            pool.wait_ge(consts_ready, 6)
            nc.gpsimd.memset(vp[:, :, :, XD:XD + 1], 1.0).then_inc(consts_ready, 1)
            nc.gpsimd.affine_select(out=ident[:], in_=ident[:], compare_op=ALU.not_equal, fill=1.0, base=0,
                                    pattern=[[-1, P]], channel_multiplier=1).then_inc(zeroed, 1)
            for v in range(2):
                nc.gpsimd.affine_select(out=mask[:, v, :], in_=mask[:, v, :], compare_op=ALU.is_ge, fill=MASKED,
                                        base=W, pattern=[[-1, KW]], channel_multiplier=1).then_inc(zeroed, 1)
            pool.wait_ge(zeroed, 6)
            nc.gpsimd.tensor_copy(ident_b[:], ident[:]).then_inc(consts_ready, 1)
            for v in range(2):
                nc.gpsimd.affine_select(out=mask[:, v, :], in_=mask[:, v, :], compare_op=ALU.is_ge, fill=MASKED,
                                        base=-1, pattern=[[1, KW]], channel_multiplier=-1).then_inc(zeroed, 1)
            pool.wait_ge(zeroed, 8)
            nc.gpsimd.memset(mask[:, 0, 0:W], MASKED).then_inc(consts_ready, 1)

            with pool.Fori(0, HP) as hp:
                for b in range(B):
                    n = hp * B + b
                    pool.wait_ge(rinv_ready, n + 1)
                    for t in range(QT):
                        cur = pr[:, b % 2, t, :, W:]
                        inv = rinv[:, b % 2, 2 * t:2 * t + 2].unsqueeze(2).to_broadcast([P, 2, KW])
                        nc.gpsimd.tensor_tensor(cur, cur, inv, ALU.mult).then_inc(probs_ready, 1)

            pool.wait_ge(c_loaded, 16)
            def values(b):
                src = cs[:, bass.ds(b * QT, QT), :].rearrange("p t (h d) -> p t h d", h=H)
                for t in range(QT):
                    nc.gpsimd.tensor_copy(vp[:, t, :, 0:XD], src[:, t]).then_inc(vp_ready, 1)

            values(0)
            with pool.Fori(1, B) as b:
                pool.wait_ge(pv_done, NG * QT * b)
                values(b)

        @block.scalar
        def _(act):
            ln_scalar(act, 0)
            for n in range(B * DC):
                b, c = n // DC, n % DC
                act.wait_ge(turned, n + 1)
                nc.scalar.activation(xnT[:, c, b * S:(b + 1) * S], ps[:, n, :], ACT.Copy).then_inc(xnT_ready, 1)

            def split_scalar(n0, turned0, scale):
                for n in range(B * DC):
                    act.wait_ge(turned, turned0 + n + 1)
                    if n0 + n >= 2:
                        act.wait_ge(parts_stored[n % 2], 48 * ((n0 + n) // 2))
                    nc.scalar.activation(part[:, n % 2, 0, :], ps[:, n, :], ACT.Copy, scale=scale).then_inc(hi_ready, 1)
                    act.wait_ge(rest1_ready, n0 + n + 1)
                    nc.scalar.activation(part[:, n % 2, 1, :], rest[:, n % 2, :], ACT.Copy).then_inc(mid_ready, 1)

            split_scalar(0, B * DC, 1.0)

            def exp_scores(n, b):
                act.wait_ge(max_ready, n + 1)
                for t in range(QT):
                    for h in range(2):
                        j = 2 * t + h
                        nc.scalar.activation(pr[:, b % 2, t, h, W:], ps[:, t, h * KW:(h + 1) * KW], ACT.Exp,
                                             bias=nmax[:, b % 2, j:j + 1],
                                             accum_out=rsum[:, b % 2, j:j + 1]).then_inc(exp_done, 1)

            def copy_q(n, b):
                act.wait_ge(q_filled, n + 1)
                bank = bank_of["q", b, 0]
                nc.scalar.activation(qa[0:DH, b % 2, :], ps[0:DH, bank, :], ACT.Copy, scale=DH ** -0.5).then_inc(q_ready, 1)
                nc.scalar.activation(qb[DH:P, b % 2, :], ps[DH:P, bank, :], ACT.Copy, scale=DH ** -0.5).then_inc(q_ready, 1)

            def copy_oT(n):
                act.wait_ge(oT_filled, n + 1)
                nc.scalar.activation(oT[:, :], ps[:, 6, :], ACT.Copy).then_inc(oT_ready, 1)

            act.wait_ge(consts_ready, 9)
            copy_q(0, 0)

            def head_pair(hp, last):
                n0 = hp * B
                for b in range(B):
                    exp_scores(n0 + b, b)
                    if b >= 1:
                        copy_oT(n0 + b - 1)
                    if b < B - 1 or not last:
                        copy_q(n0 + b + 1, (b + 1) % B)
                copy_oT(n0 + B - 1)

            with act.Fori(0, HP - 1) as hp:
                head_pair(hp, False)
            head_pair(HP - 1, True)

            ln_scalar(act, 1)
            split_scalar(B * DC, 2 * B * DC, XD ** -0.5)

            def copy_mT(n):
                act.wait_ge(m2T_filled, n + 1)
                if not isinstance(n, int) or n >= 1:
                    act.wait_ge(m_loaded, 32 * n)
                nc.scalar.activation(xmT[:, :], ps[0:2 * HG, 7, 0:S // 2].bitcast(BF16), ACT.Copy).then_inc(m2T_ready, 1)

            copy_mT(0)

            def cross_group(n, more):
                for u in range(16):
                    kt_, h = u // HG, u % HG
                    act.wait_ge(st_filled, 16 * n + u + 1)
                    if kt_ >= 2:
                        act.wait_ge(pv_done, 4 * n + kt_ - 1)
                    nc.scalar.activation(ex[:, kt_ % 2, h, :], ps[:, 4 + u % 2, :], ACT.Exp).then_inc(ex_ready, 1)
                    if u == 7 and more:
                        copy_mT(n + 1)
                act.wait_ge(pv_done, 4 * n + 4)
                nc.scalar.activation(xoT[:, :], ps[:, 6, :], ACT.Copy).then_inc(xoT_ready, 1)

            with act.Fori(0, B - 1) as b:
                for g in range(NG):
                    cross_group(b * NG + g, True)
            for g in range(NG):
                cross_group((B - 1) * NG + g, g < NG - 1)

            ln_scalar(act, 2)
            for n in range(B * DC):
                b, c = n // DC, n % DC
                act.wait_ge(turned, 3 * B * DC + n + 1)
                nc.scalar.activation(xnT[:, c, b * S:(b + 1) * S], ps[:, n, :], ACT.Copy).then_inc(xnT_ready, 1)
            act.wait_ge(e_ready, 1)
            nc.scalar.activation(pe8[:, :, :], lg[:, :, :], ACT.Exp).then_inc(exp_e_ready, 1)

            def silus(k, b):
                for m in range(FC):
                    u = (k * B + b) * FC + m
                    act.wait_ge(h_filled, u + 1)
                    if m >= 2 or not isinstance(k, int) or k or b:
                        act.wait_ge(h_ready, u - 1)
                    nc.scalar.activation(gt[:, m % 2, :], ps[:, 2 * (m % 2), :], ACT.Silu).then_inc(silu_ready, 1)

            for b in range(B):
                silus(0, b)
            with act.Fori(1, NE + 1) as k:
                for b in range(B):
                    silus(k, b)

        @block.vector
        def _(dve):
            ln_vector(dve, 0, lambda t: [(x_loaded[t // QT], 16)])

            def split_vector(n0, scale):
                for n in range(B * DC):
                    dve.wait_ge(hi_ready, n0 + n + 1)
                    nc.vector.scalar_tensor_tensor(rest[:, n % 2, :], ps[:, n, :], scale, part[:, n % 2, 0, :],
                                                   ALU.mult, ALU.subtract).then_inc(rest1_ready, 1)
                    dve.wait_ge(mid_ready, n0 + n + 1)
                    nc.vector.tensor_tensor(part[:, n % 2, 2, :], rest[:, n % 2, :], part[:, n % 2, 1, :],
                                            ALU.subtract).then_inc(parts_ready, 1)

            split_vector(0, 1.0)

            def copy_kv(n, b):
                for filled, ready, name in ((k_filled, k_ready, "k"), (v_filled, v_ready, "v")):
                    dve.wait_ge(filled, n + 1)
                    dst = kt[:, b % 2, W:] if name == "k" else vv[:, b % 2, :, :].rearrange("p t n -> p (t n)")
                    nc.vector.tensor_copy(dst, ps[:, bank_of[name, b, 0], :]).then_inc(ready, 1)

            def maxima(n, b):
                dve.wait_ge(scores_filled, QT * (n + 1))
                s = ps[:, 0:QT, 0:2 * KW].rearrange("p t (h k) -> p t h k", h=2)
                nc.vector.tensor_reduce(nmax[:, b % 2, :].rearrange("p (t h) -> p t h", h=2), s, AXX, ALU.max,
                                        negate=True).then_inc(max_ready, 1)

            def inverse_sums(n, b):
                dve.wait_ge(exp_done, 2 * QT * (n + 1))
                nc.vector.reciprocal(rinv[:, b % 2, :], rsum[:, b % 2, :]).then_inc(rinv_ready, 1)

            def copy_prT(n, b):
                for t in range(QT):
                    src = ps[:, bank_of["pT", b, t], :].rearrange("p (h k q) -> p h k q", h=2, k=2)
                    dve.wait_ge(prT_filled, QT * n + t + 1)
                    if t >= 1:
                        nc.vector.tensor_copy(prT[:, :, t - 1, P:KW], src[:, :, 0, 0:W]).then_inc(prT_ready, 1)
                    nc.vector.tensor_copy(prT[:, :, t, 0:P], src[:, :, 1, :]).then_inc(prT_ready, 1)

            def add_y(n, b):
                for i in range(2):
                    tiles = xs[:, QT * b + 2 * i:QT * b + 2 * i + 2, :].rearrange("p t d -> p (t d)")
                    dve.wait_ge(y_filled, 2 * n + i + 1)
                    nc.vector.tensor_tensor(tiles, tiles, ps[:, bank_of["y", b, i], :], ALU.add).then_inc(x1_ready, 1)

            dve.wait_ge(consts_ready, 9)
            nc.vector.sem_inc(x1_ready, 1)
            copy_kv(0, 0)

            def head_pair(hp, last):
                n0 = hp * B
                for b in range(B):
                    maxima(n0 + b, b)
                    if b >= 1:
                        copy_prT(n0 + b - 1, b - 1)
                    if b < 1:
                        copy_kv(n0 + b + 1, (b + 1) % B)
                    inverse_sums(n0 + b, b)
                    if b >= 1:
                        add_y(n0 + b - 1, b - 1)
                        if b < B - 1 or not last:
                            copy_kv(n0 + b + 1, (b + 1) % B)
                copy_prT(n0 + B - 1, B - 1)
                add_y(n0 + B - 1, B - 1)

            with dve.Fori(0, HP - 1) as hp:
                head_pair(hp, False)
            head_pair(HP - 1, True)

            ln_vector(dve, 1, lambda t: [(x1_ready, 1 + 2 * HP * B)] if t == 0 else [])
            split_vector(B * DC, XD ** -0.5)

            def cross_max(n, par):
                for u in range(8):
                    h, q2 = u // 2, u % 2
                    dve.wait_ge(xs_filled, 8 * n + u + 1)
                    nc.vector.tensor_reduce(xnm[:, par, h, 2 * q2:2 * q2 + 2], ps[:, 2 * (u % 2):2 * (u % 2) + 2, :], AXX,
                                            ALU.max, negate=True).then_inc(nmax_ready, 1)

            def cross_split_max(n, par):
                dve.wait_ge(nmax_ready, 8 * n + 8)
                nc.vector.tensor_copy(xm2[:, par, 0, :, :], xnm[:, par, :, :]).then_inc(part1_ready, 1)
                dve.wait_ge(part1_ready, n + 1)
                nc.vector.tensor_tensor(xm2[:, par, 1, :, :], xnm[:, par, :, :], xm2[:, par, 0, :, :],
                                        ALU.subtract).then_inc(m2_ready, 1)

            def cross_add(n, b, g):
                sums = ps[:, 7, :].rearrange("p (t h d) -> p t h d", t=QT, h=HG)
                dve.wait_ge(xoN_filled, n + 1)
                nc.vector.reciprocal(xr[:, :, :], sums[:, :, :, XD]).then_inc(xr_ready, 1)
                dve.wait_ge(xr_ready, n + 1)
                nc.vector.tensor_tensor(xo[:, :, :, :], sums[:, :, :, 0:XD],
                                        xr[:, :, :].unsqueeze(3).to_broadcast([P, QT, HG, XD]), ALU.mult).then_inc(xo_ready, 1)
                dve.wait_ge(xo_ready, n + 1)
                part_x = xs[:, bass.ds(b * QT, QT), g * HG * XD:(g + 1) * HG * XD]
                nc.vector.tensor_tensor(part_x, part_x, xo[:, :, :, :].rearrange("p t h d -> p t (h d)"),
                                        ALU.add).then_inc(x2_ready, 1)

            for n in range(2):
                cross_max(n, n % 2)
                cross_split_max(n, n % 2)

            def cross_group(n, b, g, more):
                if more:
                    cross_max(n + 2, g % 2)
                    cross_split_max(n + 2, g % 2)
                cross_add(n, b, g)

            with dve.Fori(0, B - 1) as b:
                for g in range(NG):
                    cross_group(b * NG + g, b, g, True)
            for g in range(NG):
                cross_group((B - 1) * NG + g, B - 1, g, g < NG - 2)

            ln_vector(dve, 2, lambda t: [(x2_ready, B * NG)] if t == 0 else [])

            steps = [0]

            def then(op):
                steps[0] += 1
                op.then_inc(route, 1)
                dve.wait_ge(route, steps[0])

            dve.wait_ge(logits_filled, 1)
            logits = ps[:, 0, 0:NT * NE].rearrange("p (t e) -> p t e", e=NE)
            then(nc.vector.tensor_reduce(lmax[:, :], logits, AXX, ALU.max))
            nc.vector.tensor_tensor(lg[:, :, :], logits, lmax[:, :].unsqueeze(2).to_broadcast([P, NT, NE]),
                                    ALU.subtract).then_inc(e_ready, 1)
            dve.wait_ge(exp_e_ready, 1)
            for t in range(NT):
                last = nc.vector.max(top[:, t, :], pe8[:, t, :])
            then(last)
            for t in range(NT):
                last = nc.vector.max_index(tix[:, t, :], top[:, t, :], pe8[:, t, :])
            then(last)
            then(nc.vector.tensor_copy(tixf[:, :, :], tix[:, :, 0:2]))
            then(nc.vector.tensor_tensor(gsum[:, :], top[:, :, 0], top[:, :, 1], ALU.add))
            then(nc.vector.reciprocal(gsum[:, :], gsum[:, :]))
            then(nc.vector.tensor_tensor(gate[:, :, :], top[:, :, 0:2], gsum[:, :].unsqueeze(2).to_broadcast([P, NT, 2]), ALU.mult))
            for i in range(2):
                then(nc.vector.tensor_tensor(hot[:, i, :, :], iota8[:, :].unsqueeze(1).to_broadcast([P, NT, NE]),
                                             tixf[:, :, i:i + 1].to_broadcast([P, NT, NE]), ALU.is_equal))
                then(nc.vector.tensor_tensor(hot[:, i, :, :], hot[:, i, :, :],
                                             gate[:, :, i:i + 1].to_broadcast([P, NT, NE]), ALU.mult))
            then(nc.vector.tensor_tensor(cw[:, :, :], hot[:, 0, :, :], hot[:, 1, :, :], ALU.add))

            def hidden(k, b):
                for m in range(FC):
                    dve.wait_ge(silu_ready, (k * B + b) * FC + m + 1)
                    nc.vector.tensor_tensor(ht[:, b % 2, m, :], gt[:, m % 2, :], ps[:, 2 * (m % 2) + 1, :],
                                            ALU.mult).then_inc(h_ready, 1)

            def add_expert(k, b, weight):
                for i in range(2):
                    dve.wait_ge(e_filled, 2 * (k * B + b) + i + 1)
                    for j in range(2):
                        t = QT * b + 2 * i + j
                        y = ps[:, 4 + 2 * (b % 2) + i, j * D:(j + 1) * D]
                        if weight:
                            nc.vector.scalar_tensor_tensor(xs[:, t, :], y, cw[:, t, bass.ds(k, 1)], xs[:, t, :],
                                                           ALU.mult, ALU.add).then_inc(e_added, 1)
                        else:
                            nc.vector.tensor_tensor(xs[:, t, :], xs[:, t, :], y, ALU.add).then_inc(e_added, 1)

            with dve.Fori(0, NE) as k:
                for b in range(B):
                    hidden(k, b)
                    if b >= 1:
                        add_expert(k, b - 1, True)
                add_expert(k, B - 1, True)
            for b in range(B):
                hidden(NE, b)
                if b >= 1:
                    add_expert(NE, b - 1, False)
            add_expert(NE, B - 1, False)

        @block.tensor
        def _(pe):
            pe.wait_ge(zeroed, 6)
            for n in range(B * DC):
                b, c = n // DC, n % DC
                pe.wait_ge(xn_ready, QT * (b + 1))
                turn(pe, xn, b, c, n, turned)
            pe.wait_ge(c_loaded, 16)
            for n in range(B * DC):
                pe.wait_ge(xnT_ready, n + 1)
                turn(pe, cs, n // DC, n % DC, n, turned)

            def await_bank(use, hp, last):
                for s, v in bank_left(use, hp, last):
                    pe.wait_ge(s, v)
                return ps[:, bank_of[use], :]

            def project(b, hp, last, first=False):
                if first:
                    pe.wait_ge(parts_ready, B * DC)
                pe.wait_ge(wqkv_loaded, 32 * (hp + (b == 0 and not first)) + 32)
                for s, filled in ((0, q_filled), (1, k_filled), (2, v_filled)):
                    use = ("qkv"[s], b, 0)
                    o = ps[:, bank_of[use], :] if first else await_bank(use, hp, last)
                    if s < 2:
                        for c in range(DC):
                            mm = nc.tensor.matmul(o, wqkv[:, c, s, :], xnT[:, c, b * S:(b + 1) * S], start=(c == 0), stop=(c == DC - 1))
                    else:
                        for t in range(QT):
                            for c in range(DC):
                                k0 = b * S + t * P
                                mm = nc.tensor.matmul(o[:, t * P:(t + 1) * P], xnT[:, c, k0:k0 + P], wqkv[:, c, 2, :],
                                                      start=(c == 0), stop=(c == DC - 1))
                    mm.then_inc(filled, 1)

            def scores(n, b):
                pe.wait_ge(q_ready, 2 * n + 2)
                pe.wait_ge(k_ready, n + 1)
                for t in range(QT):
                    if b >= 1:
                        pe.wait_ge(exp_done, 2 * QT * (n - 1) + 2 * t + 2)
                    for h in range(2):
                        o = ps[:, t, h * KW:(h + 1) * KW]
                        q = (qa, qb)[h][:, b % 2, t * P:(t + 1) * P]
                        nc.tensor.matmul(o, ident_b[:], mask[:, min(t, 1), :], start=True, stop=False)
                        mm = nc.tensor.matmul(o, q, kt[:, b % 2, t * P:t * P + KW], start=False, stop=True)
                    mm.then_inc(scores_filled, 1)

            def attend(n, b, hp, last):
                for t in range(QT):
                    use = ("pT", b, t)
                    pe.wait_ge(probs_ready, QT * n + t + 1)
                    bank = await_bank(use, hp, last)
                    for h in range(2):
                        for k in ((1,) if t == 0 else (0, 1)):
                            o = bank[:, (2 * h + k) * P:(2 * h + k + 1) * P]
                            mm = nc.tensor.transpose(o, pr[:, b % 2, t, h, k * P:(k + 1) * P], ident[:])
                    mm.then_inc(prT_filled, 1)
                pe.wait_ge(prT_ready, 7 * n + 7)
                pe.wait_ge(v_ready, n + 1)
                for t in range(QT):
                    w = KW if t < QT - 1 else P
                    for h in range(2):
                        mm = nc.tensor.matmul(ps[h * DH:(h + 1) * DH, 6, t * P:t * P + w], vv[:, b % 2, t, h * DH:(h + 1) * DH],
                                              prT[:, h, t, 0:w], start=(t == 0), stop=(t == QT - 1), skip_group_check=True)
                mm.then_inc(oT_filled, 1)

            def project_out(n, b, hp, last):
                pe.wait_ge(oT_ready, n + 1)
                pe.wait_ge(wo_loaded, 16 * hp + 16)
                for i in range(2):
                    bank = await_bank(("y", b, i), hp, last)
                    for j in range(2):
                        t = 2 * i + j
                        mm = nc.tensor.matmul(bank[:, j * D:(j + 1) * D], oT[:, t * P:(t + 1) * P], wo[:, :],
                                              start=True, stop=True)
                    mm.then_inc(y_filled, 1)

            pe.wait_ge(consts_ready, 9)
            project(0, 0, False, first=True)

            def head_pair(hp, last):
                n0 = hp * B
                for b in range(B):
                    scores(n0 + b, b)
                    if b >= 1:
                        attend(n0 + b - 1, b - 1, hp, last)
                        project_out(n0 + b - 1, b - 1, hp, last)
                    if b < B - 1 or not last:
                        project((b + 1) % B, hp, last)
                attend(n0 + B - 1, B - 1, hp, last)
                project_out(n0 + B - 1, B - 1, hp, last)

            with pe.Fori(0, HP - 1) as hp:
                head_pair(hp, False)
            head_pair(HP - 1, True)

            for n in range(B * DC):
                b, c = n // DC, n % DC
                pe.wait_ge(xn_ready, NT + QT * (b + 1))
                turn(pe, xn, b, c, n, turned)

            def cross_scores(n, g, u):
                h, q2 = u // 2, u % 2
                hh = HG * g + h
                if u >= 2 or not isinstance(n, int) or n > 0:
                    pe.wait_ge(nmax_ready, 8 * n + u - 1)
                for j in range(2):
                    mm = nc.tensor.matmul(ps[:, 2 * (u % 2) + j, :], qp[0:XS, hh, (2 * q2 + j) * P:(2 * q2 + j + 1) * P],
                                          kp[0:XS, hh, :], start=True, stop=True)
                mm.then_inc(xs_filled, 1)

            def turn_max(n, par, left=0):
                pe.wait_ge(m2_ready, n + 1)
                if left:
                    pe.wait_ge(x2_ready, left)
                for t in range(QT):
                    o = ps[0:2 * HG, 7, t * P // 2:(t + 1) * P // 2].bitcast(BF16)
                    src = xm2[:, par, :, :, t].rearrange("p i h -> p (i h)")
                    mm = nc.tensor.transpose(o, src, ident_b[:])
                mm.then_inc(m2T_filled, 1)

            def cross_exp_scores(n, g, u):
                k, h = u // HG, u % HG
                if u >= 2:
                    pe.wait_ge(ex_ready, 16 * n + u - 1)
                mm = nc.tensor.matmul(ps[:, 4 + u % 2, :], kp[:, HG * g + h, k * P:(k + 1) * P], qp[:, HG * g + h, :],
                                      start=True, stop=True)
                mm.then_inc(st_filled, 1)

            def cross_values(n, g, k):
                pe.wait_ge(ex_ready, 16 * n + 4 * k + 4)
                for h in range(HG):
                    mm = nc.tensor.matmul(ps[32 * h:32 * h + 32, 6, :], vp[:, k, HG * g + h, :], ex[:, k % 2, h, :],
                                          start=(k == 0), stop=(k == QT - 1), skip_group_check=True)
                mm.then_inc(pv_done, 1)

            pe.wait_ge(parts_ready, 2 * B * DC)
            for n in range(2):
                pe.wait_ge(split_loaded[n], 16 * 9)
                for u in range(8):
                    cross_scores(n, n, u)
            turn_max(0, 0)

            def cross_group(n, b, g, more, more_max):
                if more:
                    pe.wait_ge(split_loaded[(g + 2) % NG], 16 * 9 * (b + 1 + (g + 2) // NG))
                pe.wait_ge(m_loaded, 32 * (n + 1))
                if g == 0:
                    pe.wait_ge(vp_ready, QT * (b + 1))
                for u in range(8):
                    if more:
                        cross_scores(n + 2, (g + 2) % NG, u)
                    if u == 3 and more_max:
                        turn_max(n + 1, (g + 1) % 2, left=0 if more else n)
                    cross_exp_scores(n, g, 2 * u)
                    cross_exp_scores(n, g, 2 * u + 1)
                    if u in (3, 5, 7):
                        cross_values(n, g, (u - 3) // 2)
                cross_values(n, g, 3)
                pe.wait_ge(xoT_ready, n + 1)
                pe.wait_ge(m2T_ready, n + 2 if more_max else n + 1)
                if not more_max:
                    pe.wait_ge(x2_ready, n)
                for t in range(QT):
                    mm = nc.tensor.transpose(ps[:, 7, t * P:(t + 1) * P], xoT[:, t * P:(t + 1) * P], ident[:])
                mm.then_inc(xoN_filled, 1)

            with pe.Fori(0, B - 1) as b:
                for g in range(NG):
                    cross_group(b * NG + g, b, g, True, True)
            for g in range(NG):
                cross_group((B - 1) * NG + g, B - 1, g, g < NG - 2, g < NG - 1)

            for n in range(B * DC):
                b, c = n // DC, n % DC
                pe.wait_ge(xn_ready, 2 * NT + QT * (b + 1))
                turn(pe, xn, b, c, n, turned)
            pe.wait_ge(wr_loaded, 16)
            pe.wait_ge(xnT_ready, 2 * B * DC)
            for t in range(NT):
                for c in range(DC):
                    mm = nc.tensor.matmul(ps[:, 0, t * NE:(t + 1) * NE], xnT[:, c, t * P:(t + 1) * P], wr[:, c, :],
                                          start=(c == 0), stop=(c == DC - 1))
            mm.then_inc(logits_filled, 1)
            pe.wait_ge(e_ready, 1)

            def expert_hidden(k, par, b, started):
                for m in range(FC):
                    u = (k * B + b) * FC + m
                    if m >= 2 or b or started:
                        pe.wait_ge(h_ready, u - 1)
                    for w, bank in ((wa, 2 * (m % 2)), (wb, 2 * (m % 2) + 1)):
                        for c in range(DC):
                            mm = nc.tensor.matmul(ps[:, bank, :], w[:, par, c, m * P:(m + 1) * P], xnT[:, c, b * S:(b + 1) * S],
                                                  start=(c == 0), stop=(c == DC - 1))
                    mm.then_inc(h_filled, 1)

            def expert_out(k, par, b, started):
                pe.wait_ge(h_ready, (k * B + b + 1) * FC)
                if b >= 2 or started:
                    pe.wait_ge(e_added, 4 * (k * B + b) - 4)
                for i in range(2):
                    for j in range(2):
                        t = 2 * i + j
                        for m in range(FC):
                            mm = nc.tensor.matmul(ps[:, 4 + 2 * (b % 2) + i, j * D:(j + 1) * D], ht[:, b % 2, m, t * P:(t + 1) * P],
                                                  wc[:, par, m, :], start=(m == 0), stop=(m == FC - 1))
                    mm.then_inc(e_filled, 1)

            def expert(k, par, loads, started):
                pe.wait_ge(expert_loaded[par], 48 * loads)
                for b in range(B):
                    expert_hidden(k, par, b, started)
                    if b >= 1:
                        expert_out(k, par, b - 1, started)
                expert_out(k, par, B - 1, started)

            expert(0, 0, 1, False)
            expert(1, 1, 1, True)
            with pe.Fori(1, NE // 2) as i:
                for j in range(2):
                    expert(2 * i + j, j, i + 1, True)
            expert(NE, 0, NE // 2 + 1, True)


_INS = ["x", "ctx_1024", "L0_attn_w_qkv", "L0_attn_w_out", "L0_ffn_w_router", "L0_ffn_w1", "L0_ffn_w3", "L0_ffn_w2",
        "L0_ffn_sw1", "L0_ffn_sw3", "L0_ffn_sw2"]
_OUTS = [((4, 512, 256), "float32")]


def kernel(**inputs):
    import numpy as _np
    import concourse.bacc as _bacc
    from concourse import mybir as _mybir
    from concourse.bass_utils import run_bass_kernel_spmd as _run

    nc = _bacc.Bacc("TRN2", target_bir_lowering=False, num_devices=1)
    arrays, args = {}, []
    for name in _INS:
        a = _np.ascontiguousarray(inputs[name])
        arrays[f"in_{name}_dram"] = a
        args.append(nc.dram_tensor(f"in_{name}_dram", a.shape, _mybir.dt.from_np(a.dtype), kind="ExternalInput").ap())
    for i, (shape, dtype) in enumerate(_OUTS):
        dt = _mybir.dt.from_np(_np.dtype(dtype))
        args.append(nc.dram_tensor(f"out_{i}_dram", shape, dt, kind="ExternalOutput").ap())
    decoder_layer(nc, *args)
    r = _run(nc, [arrays], core_ids=[0])
    return r.results[0]["out_0_dram"]
```

```python
from contextlib import ExitStack

import concourse.bass as bass
import concourse.mybir as mybir
from concourse.alu_op_type import AluOpType as ALU

F32 = mybir.dt.float32
BF16 = mybir.dt.bfloat16
U32 = mybir.dt.uint32
I32 = mybir.dt.int32
ACT = mybir.ActivationFunctionType
AXX = mybir.AxisListType.X

P = 128
B, S, D = 4, 512, 256
T = B * S
NT = T // P
QT = S // P
DC = D // P
H = 16
DH = 64
HP = H * DH // P
W = 64
KW = W + P
XD = D // H
XS = 6 * XD
HG = 4
NG = H // HG
NE = 8
F = 512
FC = F // P
TOP = 2
MT = (TOP * T + NE * (P - 1)) // P
assert MT % 2 == 1
SLOTS = MT * P
SHARED_FIRST = 2
EPS = 1e-5
MASKED = -3.0e38
RING = (4, 5, 7)


def decoder_layer(nc, x, ctx, w_qkv, w_out, w_router, w1, w3, w2, sw1, sw3, sw2, out):
    with ExitStack() as es:
        def sb(name, shape, dt=F32):
            return es.enter_context(nc.sbuf_tensor(name, shape, dt))

        def sem(name):
            return es.enter_context(nc.semaphore(name))

        ps = es.enter_context(nc.psum_tensor("ps", [P, 8, 512], F32))

        xs = sb("xs", [P, NT, D])
        xn = sb("xn", [P, NT, D])
        xnT = sb("xnT", [P, DC, T])
        stats = sb("stats", [P, NT, 6])
        mv = sb("mv", [P, NT, 2])
        std = sb("std", [P, NT])
        rstd = sb("rstd", [P, NT])
        ident = sb("ident", [P, P])
        ident_b = sb("ident_b", [P, P], BF16)
        mask = sb("mask", [P, 2, KW], BF16)

        WREG = NE * DC * F
        region_a = sb("region_a", [P, 2 * WREG])
        region_b = sb("region_b", [P, 19200])

        def planner(region):
            at = [0]

            def view(*shape, dt=F32):
                n = 1
                for k in shape:
                    n *= k
                words = n if dt is F32 else n // 2
                ap = region[:, at[0]:at[0] + words]
                at[0] += words
                assert at[0] <= region.shape[1], (at[0], region.shape)
                ap = ap if dt is F32 else ap.bitcast(dt)
                names = "abcd"[:len(shape)]
                return ap.rearrange(f"p ({' '.join(names)}) -> p {' '.join(names)}", **dict(zip(names[1:], shape[1:])))
            return view

        view = planner(region_a)
        wqkv = view(DC, 3, P)
        wo = view(D)
        qa = view(2, S)
        qb = view(2, S)
        kt = view(2, W + S)
        vv = view(2, QT, P)
        pr = region_a[:, 8192:8192 + 4096].rearrange("p (i t h k) -> p i t h k", i=2, t=QT, h=2)
        prT = view(2, QT, KW)
        oT = view(S)
        nmax = sb("nmax", [P, 2, 2 * QT])
        rsum = sb("rsum", [P, 2, 2 * QT])
        rinv = sb("rinv", [P, 2, 2 * QT])

        view = planner(region_b)
        cs = view(NT, D)
        qp = view(H, S, dt=BF16)
        kp = view(H, S, dt=BF16)
        vp = view(QT, H, 32)
        view_split = planner(region_b)
        view_split(3 * NT * D + 2048)
        part = view_split(2, 3, S, dt=BF16)
        rest = view_split(2, S)
        ex = view(2, HG, S)
        xoT = view(S)
        xnm = sb("xnm", [P, 2, HG, QT])
        xm2 = sb("xm2", [P, 2, 2, HG, QT], BF16)
        xmT = sb("xmT", [2 * HG, S], BF16)
        xr = sb("xr", [P, QT, HG])
        xo = sb("xo", [P, QT, HG, XD])

        view = planner(region_a)
        w1s = view(NE, DC * F)
        w3s = view(NE, DC * F)
        view = planner(region_b)
        w2s = view(NE, FC * D)
        wa = view(DC, F)
        wb = view(DC, F)
        wc = view(FC, D)
        gt = view(2, S)
        ht = view(2, FC, S)
        xg, xgT = xn[:, 0:2, :], xn[:, 2:4, :].rearrange("p i (c t) -> p i c t", c=DC)
        yrow, yg = xn[:, 4:6, :], xn[:, 6:10, :]
        gs = gt
        hid = ht[:, 0, 0:2, :]
        hidT = ht[:, 0, 2:4, :].rearrange("p i (m t) -> p i m t", m=FC)
        wr = sb("wr", [P, DC, NE])
        lmax = sb("lmax", [P, NT])
        lg = sb("lg", [P, NT, NE])
        top = sb("top", [P, NT, 8])
        tix = sb("tix", [P, NT, 8], U32)
        tixf = sb("tixf", [P, NT, TOP])
        gsum = sb("gsum", [P, NT])
        gate = sb("gate", [P, NT, TOP])
        iota8 = sb("iota8", [P, NE])
        iota_mt = sb("iota_mt", [1, MT])
        hot = sb("hot", [P, TOP, NT, NE])
        sel = sb("sel", [P, NT, NE])
        before = sb("before", [P, P])
        ones = sb("ones", [P, P])
        run = sb("run", [P, 2, 8 + NT, NE])
        tiles_f = sb("tiles_f", [P, NE])
        tiles_i = sb("tiles_i", [P, NE], I32)
        ends = sb("ends", [P, 2, 4 + NE])
        slot_e = sb("slot_e", [P, NT, NE])
        slot_f = sb("slot_f", [P, TOP, NT])
        slot = sb("slot", [P, TOP, NT], U32)
        owner_e = sb("owner_e", [1, MT, NE - 1])
        owner_f = sb("owner_f", [1, MT])
        owner = sb("owner", [1, MT], I32)
        zrow = sb("zrow", [P, D])

        xsort = nc.dram_tensor("xsort", (SLOTS, D), F32, kind="Internal").ap()
        ysort = nc.dram_tensor("ysort", (SLOTS, D), F32, kind="Internal").ap()
        scr_q = nc.dram_tensor("scr_q", (H, 3, XD, T), BF16, kind="Internal").ap()
        scr_k = nc.dram_tensor("scr_k", (H, 3, XD, T), BF16, kind="Internal").ap()

        x_loaded = [sem(f"x_loaded{b}") for b in range(B)]
        c_loaded = sem("c_loaded")
        stats_ready, mv_ready, var_ready, std_ready = sem("stats_ready"), sem("mv_ready"), sem("var_ready"), sem("std_ready")
        rstd_ready, xn_ready = sem("rstd_ready"), sem("xn_ready")
        turned, xnT_ready = sem("turned"), sem("xnT_ready")
        zeroed, consts_ready = sem("zeroed"), sem("consts_ready")
        hi_ready, rest1_ready, mid_ready, parts_ready = sem("hi_ready"), sem("rest1_ready"), sem("mid_ready"), sem("parts_ready")
        parts_stored = [sem("parts_stored0"), sem("parts_stored1")]

        wqkv_loaded, wo_loaded = sem("wqkv_loaded"), sem("wo_loaded")
        q_filled, k_filled, v_filled = sem("q_filled"), sem("k_filled"), sem("v_filled")
        q_ready, k_ready, v_ready = sem("q_ready"), sem("k_ready"), sem("v_ready")
        scores_filled, max_ready, exp_done = sem("scores_filled"), sem("max_ready"), sem("exp_done")
        rinv_ready, probs_ready = sem("rinv_ready"), sem("probs_ready")
        prT_filled, prT_ready = sem("prT_filled"), sem("prT_ready")
        oT_filled, oT_ready, y_filled = sem("oT_filled"), sem("oT_ready"), sem("y_filled")
        x1_ready = sem("x1_ready")

        split_loaded = [sem(f"split_loaded{g}") for g in range(NG)]
        vp_ready = sem("vp_ready")
        xs_filled = sem("xs_filled")
        nmax_ready, part1_ready, m2_ready = sem("nmax_ready"), sem("part1_ready"), sem("m2_ready")
        m2T_filled, m2T_ready, m_loaded = sem("m2T_filled"), sem("m2T_ready"), sem("m_loaded")
        st_filled, ex_ready, pv_done = sem("st_filled"), sem("ex_ready"), sem("pv_done")
        xoT_ready, xoN_filled, xr_ready, xo_ready, x2_ready = sem("xoT_ready"), sem("xoN_filled"), sem("xr_ready"), sem("xo_ready"), sem("x2_ready")

        wr_loaded, logits_filled, route = sem("wr_loaded"), sem("logits_filled"), sem("route")
        e_ready, exp_e_ready, counts_filled, sel_ready = sem("e_ready"), sem("exp_e_ready"), sem("counts_filled"), sem("sel_ready")
        owner_ready, slots_ready, xsort_zeroed, xsorted = sem("owner_ready"), sem("slots_ready"), sem("xsort_zeroed"), sem("xsorted")
        w13_loaded, w2_loaded, shared_loaded = sem("w13_loaded"), sem("w2_loaded"), sem("shared_loaded")
        h_filled, silu_ready, h_ready = sem("h_filled"), sem("silu_ready"), sem("h_ready")
        e_filled, e_added, x3_stored = sem("e_filled"), sem("e_added"), sem("x3_stored")
        rows_loaded = [sem("rows_loaded0"), sem("rows_loaded1")]
        rowsT_filled, rowsT_ready, g13_filled, g_ready = sem("rowsT_filled"), sem("rowsT_ready"), sem("g13_filled"), sem("g_ready")
        hid_ready, hidT_filled, hidT_ready, yrow_filled, yrow_ready = sem("hid_ready"), sem("hidT_filled"), sem("hidT_ready"), sem("yrow_filled"), sem("yrow_ready")
        y_stored = [sem("y_stored0"), sem("y_stored1")]
        y_gathered = [sem(f"y_gathered{i}") for i in range(4)]
        combined = sem("combined")

        x_in = x.rearrange("b (t p) d -> b p t d", p=P)
        c_in = ctx.rearrange("b (t p) d -> p (b t) d", p=P)
        y_out = out.rearrange("b (t p) d -> b p t d", p=P)
        wqkv_in = w_qkv.rearrange("(c p) (s h n) -> c p s h n", p=P, s=3, h=HP)
        wo_in = w_out.rearrange("(h p) n -> h p n", p=P)

        w1_in, w3_in = (w.rearrange("e (c p) f -> e p c f", p=P) for w in (w1, w3))
        w2_in = w2.rearrange("e (c p) d -> p e c d", p=P)
        xsort_t, ysort_t = (r.rearrange("(j p) d -> j p d", p=P) for r in (xsort, ysort))
        sw1_in, sw3_in, sw2_in = (w.rearrange("(c p) f -> p c f", p=P) for w in (sw1, sw3, sw2))

        def ln_vector(dve, n, x_waits):
            for t in range(NT):
                for s, v in x_waits(t):
                    dve.wait_ge(s, v)
                nc.vector.bn_stats(stats[:, t, :], xs[:, t, :]).then_inc(stats_ready, 1)
            dve.wait_ge(stats_ready, NT * (n + 1))
            for t in range(NT):
                nc.vector.bn_aggr(mv[:, t, :], stats[:, t, :]).then_inc(mv_ready, 1)
            dve.wait_ge(mv_ready, NT * (n + 1))
            nc.vector.tensor_scalar(rstd[:, :], mv[:, :, 1], EPS, None, ALU.add).then_inc(var_ready, 1)
            dve.wait_ge(std_ready, n + 1)
            nc.vector.reciprocal(rstd[:, :], std[:, :]).then_inc(rstd_ready, 1)
            dve.wait_ge(rstd_ready, n + 1)
            for t in range(NT):
                nc.vector.tensor_scalar(xn[:, t, :], xs[:, t, :], mv[:, t, 0:1], rstd[:, t:t + 1],
                                        ALU.subtract, ALU.mult).then_inc(xn_ready, 1)

        def ln_scalar(act, n):
            act.wait_ge(var_ready, n + 1)
            nc.scalar.activation(std[:, :], rstd[:, :], ACT.Sqrt).then_inc(std_ready, 1)

        def turn(pe, src, b, c, bank, done):
            for t in range(QT):
                mm = nc.tensor.transpose(ps[:, bank, t * P:(t + 1) * P], src[:, QT * b + t, c * P:(c + 1) * P], ident[:])
            mm.then_inc(done, 1)

        order = []
        for b in range(B):
            if b >= 1:
                order += [("pT", b - 1, t) for t in range(QT)] + [("y", b - 1, i) for i in range(2)]
            order += [(s, (b + 1) % B, 0) for s in "qkv"]
        order += [("pT", B - 1, t) for t in range(QT)] + [("y", B - 1, i) for i in range(2)]
        bank_of = {use: RING[n % 3] for n, use in enumerate(order)}

        def bank_left(use, hp, last):
            at = order.index(use)
            if last and order[at - 3][0] in "qkv" and order[at - 3][1] == 0:
                at -= 3
            if at < 3:
                return [(x1_ready, 1 + 2 * B * hp), (v_ready, B * hp + 1)]
            name, b, i = order[at - 3]
            n = (hp + 1) * B if name in "qkv" and b == 0 else hp * B + b
            return {"q": [(q_ready, 2 * n + 2)], "k": [(k_ready, n + 1)], "v": [(v_ready, n + 1)],
                    "pT": [(prT_ready, 7 * n + 2 * i + 1)], "y": [(x1_ready, 2 * n + i + 2)]}[name]

        def slot_steps(eng, step):
            def two(i, last=False):
                step(2 * i + 1, 1, True, i)
                step(2 * i + 2, 0, not last, i)

            two(0)
            with eng.Fori(1, MT // 2 - 1) as i:
                two(i)
            two(MT // 2 - 1, last=True)

        block = es.enter_context(nc.Block())

        @block.sync
        def _(sp):
            for b in range(B):
                sp.dma_start(xs[:, QT * b:QT * (b + 1), :], x_in[b]).then_inc(x_loaded[b], 16)
            for c in range(DC):
                sp.dma_start(wqkv[:, c, :, :], wqkv_in[c, :, :, 0, :]).then_inc(wqkv_loaded, 16)
            sp.dma_start(wo[:, :], wo_in[0]).then_inc(wo_loaded, 16)
            sp.dma_start(cs[:, :, :], c_in).then_inc(c_loaded, 16)

            def store_parts(scr, n0):
                for n in range(B * DC):
                    b, c = n // DC, n % DC
                    sp.wait_ge(parts_ready, n0 + n + 1)
                    for i in range(3):
                        sp.dma_start(scr[c * 8:(c + 1) * 8, i, :, b * S:(b + 1) * S], part[:, n % 2, i, :]).then_inc(parts_stored[n % 2], 16)

            sp.wait_ge(zeroed, 1)
            sp.dma_start(xsort.rearrange("(j p) d -> p j d", p=P),
                         zrow[:, :].unsqueeze(1).to_broadcast([P, MT, D])).then_inc(xsort_zeroed, 16)
            store_parts(scr_k, 0)

            with sp.Fori(0, HP - 1) as hp:
                sp.wait_ge(v_filled, hp * B + B)
                for c in range(DC):
                    sp.dma_start(wqkv[:, c, :, :], wqkv_in[c, :, :, hp + 1, :]).then_inc(wqkv_loaded, 16)
                sp.wait_ge(y_filled, hp * 2 * B + 2 * B)
                sp.dma_start(wo[:, :], wo_in[hp + 1]).then_inc(wo_loaded, 16)

            store_parts(scr_q, B * DC)
            for i in range(2):
                sp.wait_ge(parts_stored[i], 16 * 3 * B * DC)

            def load_split(b, g):
                hs = slice(HG * g, HG * (g + 1))
                ts = bass.ds(b * S, S)
                for rows, parts, scr, dst in ((0, (0, 1, 2), scr_q, qp), (3 * XD, (0, 1), scr_q, qp), (5 * XD, (0,), scr_q, qp)):
                    n = XD * len(parts)
                    src = scr.rearrange("h i d t -> (i d) h t")[0:n, hs, ts]
                    sp.dma_start(dst[rows:rows + n, hs, :], src).then_inc(split_loaded[g], 16)
                for seg, i in enumerate((0, 0, 0, 1, 1, 2)):
                    src = scr_k[hs, i, :, ts].rearrange("h d t -> d h t")
                    sp.dma_start(kp[XD * seg:XD * (seg + 1), hs, :], src).then_inc(split_loaded[g], 16)

            def load_max(n, g):
                sp.wait_ge(m2T_ready, n + 1)
                for i in range(2):
                    sp.dma_start(qp[XS + i:XS + i + 1, HG * g:HG * (g + 1), :], xmT[HG * i:HG * (i + 1), :]).then_inc(m_loaded, 16)

            def load_w13(e, which):
                dst, src = ((w1s, w1_in), (w3s, w3_in))[which]
                sp.dma_start(dst[:, bass.ds(e, 1), :].rearrange("p e (c f) -> p (e c) f", c=DC), src[e]).then_inc(w13_loaded, 16)

            for g in range(NG):
                load_split(0, g)
            load_max(0, 0)
            with sp.Fori(0, B - 1) as b:
                for g in range(NG):
                    n = b * NG + g
                    load_max(n + 1, (g + 1) % NG)
                    sp.wait_ge(st_filled, 16 * (n + 1))
                    load_split(b + 1, g)
                    load_w13(2 * b + g // 2, g % 2)
            for g in range(NG - 1):
                load_max((B - 1) * NG + g + 1, g + 1)

            for e in range(2 * (B - 1), NE):
                for which in range(2):
                    load_w13(e, which)
            sp.dma_start(wr[:, :, :], w_router.rearrange("(c p) e -> p c e", p=P)).then_inc(wr_loaded, 16)
            sp.wait_ge(x2_ready, B * NG)
            for dst, src in ((wa, sw1_in), (wb, sw3_in), (wc, sw2_in)):
                sp.dma_start(dst, src).then_inc(shared_loaded, 16)
            for e in range(NE):
                sp.dma_start(w2s[:, e, :].rearrange("p (c d) -> p c d", c=FC), w2_in[:, e]).then_inc(w2_loaded, 16)

            def load_rows(j, par):
                sp.dma_start(xg[:, par, :], xsort_t[j]).then_inc(rows_loaded[par], 16)

            def store_rows(j, par):
                sp.wait_ge(yrow_ready, j + 1)
                sp.dma_start(ysort_t[j], yrow[:, par, :]).then_inc(y_stored[par], 16)

            sp.wait_ge(xsorted, 16 * TOP * NT)
            load_rows(0, 0)
            load_rows(1, 1)
            sp.wait_ge(rowsT_filled, 1)
            load_rows(2, 0)
            with sp.Fori(0, (MT - 3) // 2) as i:
                for k in range(2):
                    j = 2 * i + k
                    sp.wait_ge(rowsT_filled, j + 2)
                    load_rows(j + 3, (k + 1) % 2)
                    store_rows(j, k)
            for j in range(MT - 3, MT):
                store_rows(j, j % 2)
            for b in range(B):
                sp.wait_ge(combined, 2 * QT * (b + 1))
                sp.dma_start(y_out[b], xs[:, QT * b:QT * (b + 1), :]).then_inc(x3_stored, 16)
            sp.wait_ge(x3_stored, 16 * B)

        @block.gpsimd
        def _(pool):
            nc.gpsimd.memset(zrow[:], 0.0).then_inc(zeroed, 1)
            nc.gpsimd.memset(ident[:], 0.0).then_inc(zeroed, 1)
            nc.gpsimd.memset(mask[:], 0.0).then_inc(zeroed, 1)
            nc.gpsimd.iota(iota8[:], [[1, NE]], base=0, channel_multiplier=0,
                           allow_small_or_imprecise_dtypes=True).then_inc(consts_ready, 1)
            nc.gpsimd.memset(qa[:], 0.0).then_inc(consts_ready, 1)
            nc.gpsimd.memset(qb[:], 0.0).then_inc(consts_ready, 1)
            nc.gpsimd.memset(kt[:], 0.0).then_inc(consts_ready, 1)
            nc.gpsimd.memset(pr[:, :, :, :, 0:W], 0.0).then_inc(consts_ready, 1)
            nc.gpsimd.memset(vp[:], 0.0).then_inc(zeroed, 1)
            pool.wait_ge(zeroed, 4)
            nc.gpsimd.memset(kp[XS:XS + 2, :, :], 1.0).then_inc(consts_ready, 1)
            pool.wait_ge(consts_ready, 6)
            nc.gpsimd.memset(vp[:, :, :, XD:XD + 1], 1.0).then_inc(consts_ready, 1)
            nc.gpsimd.affine_select(out=ident[:], in_=ident[:], compare_op=ALU.not_equal, fill=1.0, base=0,
                                    pattern=[[-1, P]], channel_multiplier=1).then_inc(zeroed, 1)
            for v in range(2):
                nc.gpsimd.affine_select(out=mask[:, v, :], in_=mask[:, v, :], compare_op=ALU.is_ge, fill=MASKED,
                                        base=W, pattern=[[-1, KW]], channel_multiplier=1).then_inc(zeroed, 1)
            pool.wait_ge(zeroed, 7)
            nc.gpsimd.tensor_copy(ident_b[:], ident[:]).then_inc(consts_ready, 1)
            for v in range(2):
                nc.gpsimd.affine_select(out=mask[:, v, :], in_=mask[:, v, :], compare_op=ALU.is_ge, fill=MASKED,
                                        base=-1, pattern=[[1, KW]], channel_multiplier=-1).then_inc(zeroed, 1)
            pool.wait_ge(zeroed, 9)
            nc.gpsimd.memset(mask[:, 0, 0:W], MASKED).then_inc(consts_ready, 1)
            nc.gpsimd.memset(before[:], 1.0).then_inc(zeroed, 1)
            nc.gpsimd.memset(ones[:], 1.0).then_inc(consts_ready, 1)
            nc.gpsimd.memset(run[:], 0.0).then_inc(consts_ready, 1)
            nc.gpsimd.memset(ends[:], 0.0).then_inc(consts_ready, 1)
            nc.gpsimd.iota(iota_mt[:], [[1, MT]], base=0, channel_multiplier=0,
                           allow_small_or_imprecise_dtypes=True).then_inc(consts_ready, 1)
            pool.wait_ge(zeroed, 10)
            nc.gpsimd.affine_select(out=before[:], in_=before[:], compare_op=ALU.is_gt, fill=0.0, base=0,
                                    pattern=[[1, P]], channel_multiplier=-1).then_inc(consts_ready, 1)

            with pool.Fori(0, HP) as hp:
                for b in range(B):
                    n = hp * B + b
                    pool.wait_ge(rinv_ready, n + 1)
                    for t in range(QT):
                        cur = pr[:, b % 2, t, :, W:]
                        inv = rinv[:, b % 2, 2 * t:2 * t + 2].unsqueeze(2).to_broadcast([P, 2, KW])
                        nc.gpsimd.tensor_tensor(cur, cur, inv, ALU.mult).then_inc(probs_ready, 1)

            pool.wait_ge(c_loaded, 16)
            def values(b):
                src = cs[:, bass.ds(b * QT, QT), :].rearrange("p t (h d) -> p t h d", h=H)
                for t in range(QT):
                    nc.gpsimd.tensor_copy(vp[:, t, :, 0:XD], src[:, t]).then_inc(vp_ready, 1)

            values(0)
            with pool.Fori(1, B) as b:
                pool.wait_ge(pv_done, NG * QT * b)
                values(b)

            pool.wait_ge(slots_ready, 1)
            pool.wait_ge(xsort_zeroed, 16)
            pool.wait_ge(xn_ready, 3 * NT)
            for t in range(NT):
                for i in range(TOP):
                    nc.gpsimd.indirect_dma_start(out=xsort, out_offset=bass.IndirectOffsetOnAxis(ap=slot[:, i, t:t + 1], axis=0),
                                                 in_=xn[:, t, :], in_offset=None).then_inc(xsorted, 16)
            pool.wait_ge(y_stored[0], 16 * ((MT + 1) // 2))
            pool.wait_ge(y_stored[1], 16 * (MT // 2))
            for t in range(NT):
                for i in range(TOP):
                    n = TOP * t + i
                    if n >= 4:
                        pool.wait_ge(combined, n - 3)
                    nc.gpsimd.indirect_dma_start(out=yg[:, n % 4, :], out_offset=None, in_=ysort,
                                                 in_offset=bass.IndirectOffsetOnAxis(ap=slot[:, i, t:t + 1], axis=0)).then_inc(y_gathered[n % 4], 16)

        @block.scalar
        def _(act):
            ln_scalar(act, 0)
            for n in range(B * DC):
                b, c = n // DC, n % DC
                act.wait_ge(turned, n + 1)
                nc.scalar.activation(xnT[:, c, b * S:(b + 1) * S], ps[:, n, :], ACT.Copy).then_inc(xnT_ready, 1)

            def split_scalar(n0, turned0, scale):
                for n in range(B * DC):
                    act.wait_ge(turned, turned0 + n + 1)
                    if n0 + n >= 2:
                        act.wait_ge(parts_stored[n % 2], 48 * ((n0 + n) // 2))
                    nc.scalar.activation(part[:, n % 2, 0, :], ps[:, n, :], ACT.Copy, scale=scale).then_inc(hi_ready, 1)
                    act.wait_ge(rest1_ready, n0 + n + 1)
                    nc.scalar.activation(part[:, n % 2, 1, :], rest[:, n % 2, :], ACT.Copy).then_inc(mid_ready, 1)

            split_scalar(0, B * DC, 1.0)

            def exp_scores(n, b):
                act.wait_ge(max_ready, n + 1)
                for t in range(QT):
                    for h in range(2):
                        j = 2 * t + h
                        nc.scalar.activation(pr[:, b % 2, t, h, W:], ps[:, t, h * KW:(h + 1) * KW], ACT.Exp,
                                             bias=nmax[:, b % 2, j:j + 1],
                                             accum_out=rsum[:, b % 2, j:j + 1]).then_inc(exp_done, 1)

            def copy_q(n, b):
                act.wait_ge(q_filled, n + 1)
                bank = bank_of["q", b, 0]
                nc.scalar.activation(qa[0:DH, b % 2, :], ps[0:DH, bank, :], ACT.Copy, scale=DH ** -0.5).then_inc(q_ready, 1)
                nc.scalar.activation(qb[DH:P, b % 2, :], ps[DH:P, bank, :], ACT.Copy, scale=DH ** -0.5).then_inc(q_ready, 1)

            def copy_oT(n):
                act.wait_ge(oT_filled, n + 1)
                nc.scalar.activation(oT[:, :], ps[:, 6, :], ACT.Copy).then_inc(oT_ready, 1)

            act.wait_ge(consts_ready, 9)
            copy_q(0, 0)

            def head_pair(hp, last):
                n0 = hp * B
                for b in range(B):
                    exp_scores(n0 + b, b)
                    if b >= 1:
                        copy_oT(n0 + b - 1)
                    if b < B - 1 or not last:
                        copy_q(n0 + b + 1, (b + 1) % B)
                copy_oT(n0 + B - 1)

            with act.Fori(0, HP - 1) as hp:
                head_pair(hp, False)
            head_pair(HP - 1, True)

            ln_scalar(act, 1)
            split_scalar(B * DC, 2 * B * DC, XD ** -0.5)

            def copy_mT(n):
                act.wait_ge(m2T_filled, n + 1)
                if not isinstance(n, int) or n >= 1:
                    act.wait_ge(m_loaded, 32 * n)
                nc.scalar.activation(xmT[:, :], ps[0:2 * HG, 7, 0:S // 2].bitcast(BF16), ACT.Copy).then_inc(m2T_ready, 1)

            copy_mT(0)

            def cross_group(n, more):
                for u in range(16):
                    kt_, h = u // HG, u % HG
                    act.wait_ge(st_filled, 16 * n + u + 1)
                    if kt_ >= 2:
                        act.wait_ge(pv_done, 4 * n + kt_ - 1)
                    nc.scalar.activation(ex[:, kt_ % 2, h, :], ps[:, 4 + u % 2, :], ACT.Exp).then_inc(ex_ready, 1)
                    if u == 7 and more:
                        copy_mT(n + 1)
                act.wait_ge(pv_done, 4 * n + 4)
                nc.scalar.activation(xoT[:, :], ps[:, 6, :], ACT.Copy).then_inc(xoT_ready, 1)

            with act.Fori(0, B - 1) as b:
                for g in range(NG):
                    cross_group(b * NG + g, True)
            for g in range(NG):
                cross_group((B - 1) * NG + g, g < NG - 1)

            ln_scalar(act, 2)
            for n in range(B * DC):
                b, c = n // DC, n % DC
                act.wait_ge(turned, 3 * B * DC + n + 1)
                nc.scalar.activation(xnT[:, c, b * S:(b + 1) * S], ps[:, n, :], ACT.Copy).then_inc(xnT_ready, 1)
            act.wait_ge(e_ready, 1)
            nc.scalar.activation(lg[:, :, :], lg[:, :, :], ACT.Exp).then_inc(exp_e_ready, 1)

            def silus(b, prior=0):
                for m in range(FC):
                    u = b * FC + m
                    act.wait_ge(h_filled, u + 1)
                    if u >= 2:
                        act.wait_ge(h_ready, u - 1)
                    nc.scalar.activation(gt[:, m % 2, :], ps[:, 2 * (m % 2), :], ACT.Silu).then_inc(silu_ready, 1)

            for b in range(SHARED_FIRST):
                silus(b)

            def copy_rowsT(j, par):
                act.wait_ge(rowsT_filled, j + 1)
                nc.scalar.activation(xgT[:, par, :, :].rearrange("p c t -> p (c t)"), ps[:, 4, 0:D], ACT.Copy).then_inc(rowsT_ready, 1)

            def silu_rows(j, par):
                act.wait_ge(g13_filled, j + 1)
                nc.scalar.activation(gs[:, par, :], ps[:, 2 * par, :], ACT.Silu).then_inc(g_ready, 1)

            def copy_y(j, par, i):
                act.wait_ge(yrow_filled, j + 1)
                if not isinstance(i, int) or i > 0:
                    act.wait_ge(y_stored[par], 16 * i)
                nc.scalar.activation(yrow[:, par, :], ps[:, 6 + par, 0:D], ACT.Copy).then_inc(yrow_ready, 1)

            copy_rowsT(0, 0)
            copy_rowsT(1, 1)
            silu_rows(0, 0)
            slot_steps(act, lambda j, par, more, i: (copy_rowsT(j + 1, 1 - par) if more else None, silu_rows(j, par), copy_y(j - 1, 1 - par, i)))
            copy_y(MT - 1, 0, MT // 2)
            for b in range(SHARED_FIRST, B):
                silus(b)

        @block.vector
        def _(dve):
            ln_vector(dve, 0, lambda t: [(x_loaded[t // QT], 16)])

            def split_vector(n0, scale):
                for n in range(B * DC):
                    dve.wait_ge(hi_ready, n0 + n + 1)
                    nc.vector.scalar_tensor_tensor(rest[:, n % 2, :], ps[:, n, :], scale, part[:, n % 2, 0, :],
                                                   ALU.mult, ALU.subtract).then_inc(rest1_ready, 1)
                    dve.wait_ge(mid_ready, n0 + n + 1)
                    nc.vector.tensor_tensor(part[:, n % 2, 2, :], rest[:, n % 2, :], part[:, n % 2, 1, :],
                                            ALU.subtract).then_inc(parts_ready, 1)

            split_vector(0, 1.0)

            def copy_kv(n, b):
                for filled, ready, name in ((k_filled, k_ready, "k"), (v_filled, v_ready, "v")):
                    dve.wait_ge(filled, n + 1)
                    dst = kt[:, b % 2, W:] if name == "k" else vv[:, b % 2, :, :].rearrange("p t n -> p (t n)")
                    nc.vector.tensor_copy(dst, ps[:, bank_of[name, b, 0], :]).then_inc(ready, 1)

            def maxima(n, b):
                dve.wait_ge(scores_filled, QT * (n + 1))
                s = ps[:, 0:QT, 0:2 * KW].rearrange("p t (h k) -> p t h k", h=2)
                nc.vector.tensor_reduce(nmax[:, b % 2, :].rearrange("p (t h) -> p t h", h=2), s, AXX, ALU.max,
                                        negate=True).then_inc(max_ready, 1)

            def inverse_sums(n, b):
                dve.wait_ge(exp_done, 2 * QT * (n + 1))
                nc.vector.reciprocal(rinv[:, b % 2, :], rsum[:, b % 2, :]).then_inc(rinv_ready, 1)

            def copy_prT(n, b):
                for t in range(QT):
                    src = ps[:, bank_of["pT", b, t], :].rearrange("p (h k q) -> p h k q", h=2, k=2)
                    dve.wait_ge(prT_filled, QT * n + t + 1)
                    if t >= 1:
                        nc.vector.tensor_copy(prT[:, :, t - 1, P:KW], src[:, :, 0, 0:W]).then_inc(prT_ready, 1)
                    nc.vector.tensor_copy(prT[:, :, t, 0:P], src[:, :, 1, :]).then_inc(prT_ready, 1)

            def add_y(n, b):
                for i in range(2):
                    tiles = xs[:, QT * b + 2 * i:QT * b + 2 * i + 2, :].rearrange("p t d -> p (t d)")
                    dve.wait_ge(y_filled, 2 * n + i + 1)
                    nc.vector.tensor_tensor(tiles, tiles, ps[:, bank_of["y", b, i], :], ALU.add).then_inc(x1_ready, 1)

            dve.wait_ge(consts_ready, 9)
            nc.vector.sem_inc(x1_ready, 1)
            copy_kv(0, 0)

            def head_pair(hp, last):
                n0 = hp * B
                for b in range(B):
                    maxima(n0 + b, b)
                    if b >= 1:
                        copy_prT(n0 + b - 1, b - 1)
                    if b < 1:
                        copy_kv(n0 + b + 1, (b + 1) % B)
                    inverse_sums(n0 + b, b)
                    if b >= 1:
                        add_y(n0 + b - 1, b - 1)
                        if b < B - 1 or not last:
                            copy_kv(n0 + b + 1, (b + 1) % B)
                copy_prT(n0 + B - 1, B - 1)
                add_y(n0 + B - 1, B - 1)

            with dve.Fori(0, HP - 1) as hp:
                head_pair(hp, False)
            head_pair(HP - 1, True)

            ln_vector(dve, 1, lambda t: [(x1_ready, 1 + 2 * HP * B)] if t == 0 else [])
            split_vector(B * DC, XD ** -0.5)

            def cross_max(n, par):
                for u in range(8):
                    h, q2 = u // 2, u % 2
                    dve.wait_ge(xs_filled, 8 * n + u + 1)
                    nc.vector.tensor_reduce(xnm[:, par, h, 2 * q2:2 * q2 + 2], ps[:, 2 * (u % 2):2 * (u % 2) + 2, :], AXX,
                                            ALU.max, negate=True).then_inc(nmax_ready, 1)

            def cross_split_max(n, par):
                dve.wait_ge(nmax_ready, 8 * n + 8)
                nc.vector.tensor_copy(xm2[:, par, 0, :, :], xnm[:, par, :, :]).then_inc(part1_ready, 1)
                dve.wait_ge(part1_ready, n + 1)
                nc.vector.tensor_tensor(xm2[:, par, 1, :, :], xnm[:, par, :, :], xm2[:, par, 0, :, :],
                                        ALU.subtract).then_inc(m2_ready, 1)

            def cross_add(n, b, g):
                sums = ps[:, 7, :].rearrange("p (t h d) -> p t h d", t=QT, h=HG)
                dve.wait_ge(xoN_filled, n + 1)
                nc.vector.reciprocal(xr[:, :, :], sums[:, :, :, XD]).then_inc(xr_ready, 1)
                dve.wait_ge(xr_ready, n + 1)
                nc.vector.tensor_tensor(xo[:, :, :, :], sums[:, :, :, 0:XD],
                                        xr[:, :, :].unsqueeze(3).to_broadcast([P, QT, HG, XD]), ALU.mult).then_inc(xo_ready, 1)
                dve.wait_ge(xo_ready, n + 1)
                part_x = xs[:, bass.ds(b * QT, QT), g * HG * XD:(g + 1) * HG * XD]
                nc.vector.tensor_tensor(part_x, part_x, xo[:, :, :, :].rearrange("p t h d -> p t (h d)"),
                                        ALU.add).then_inc(x2_ready, 1)

            for n in range(2):
                cross_max(n, n % 2)
                cross_split_max(n, n % 2)

            def cross_group(n, b, g, more):
                if more:
                    cross_max(n + 2, g % 2)
                    cross_split_max(n + 2, g % 2)
                cross_add(n, b, g)

            with dve.Fori(0, B - 1) as b:
                for g in range(NG):
                    cross_group(b * NG + g, b, g, True)
            for g in range(NG):
                cross_group((B - 1) * NG + g, B - 1, g, g < NG - 2)

            ln_vector(dve, 2, lambda t: [(x2_ready, B * NG)] if t == 0 else [])

            steps = [0]

            def then(op):
                steps[0] += 1
                op.then_inc(route, 1)
                dve.wait_ge(route, steps[0])

            dve.wait_ge(consts_ready, 14)
            dve.wait_ge(logits_filled, 1)
            logits = ps[:, 7, 0:NT * NE].rearrange("p (t e) -> p t e", e=NE)
            then(nc.vector.tensor_reduce(lmax[:, :], logits, AXX, ALU.max))
            nc.vector.tensor_tensor(lg[:, :, :], logits, lmax[:, :].unsqueeze(2).to_broadcast([P, NT, NE]),
                                    ALU.subtract).then_inc(e_ready, 1)
            dve.wait_ge(exp_e_ready, 1)
            for t in range(NT):
                last = nc.vector.max(top[:, t, :], lg[:, t, :])
            then(last)
            for t in range(NT):
                last = nc.vector.max_index(tix[:, t, :], top[:, t, :], lg[:, t, :])
            then(last)
            then(nc.vector.tensor_copy(tixf[:, :, :], tix[:, :, 0:TOP]))
            for i in range(TOP):
                last = nc.vector.tensor_tensor(hot[:, i, :, :], iota8[:, :].unsqueeze(1).to_broadcast([P, NT, NE]),
                                               tixf[:, :, i:i + 1].to_broadcast([P, NT, NE]), ALU.is_equal)
            then(last)
            nc.vector.tensor_tensor(sel[:, :, :], hot[:, 0, :, :], hot[:, 1, :, :], ALU.add).then_inc(sel_ready, 1)
            then(nc.vector.tensor_tensor(gsum[:, :], top[:, :, 0], top[:, :, 1], ALU.add))
            then(nc.vector.reciprocal(gsum[:, :], gsum[:, :]))
            then(nc.vector.tensor_tensor(gate[:, :, :], top[:, :, 0:TOP], gsum[:, :].unsqueeze(2).to_broadcast([P, NT, TOP]), ALU.mult))

            def hidden(b):
                for m in range(FC):
                    dve.wait_ge(silu_ready, b * FC + m + 1)
                    nc.vector.tensor_tensor(ht[:, b % 2, m, :], gt[:, m % 2, :], ps[:, 2 * (m % 2) + 1, :],
                                            ALU.mult).then_inc(h_ready, 1)

            hidden(0)
            dve.wait_ge(counts_filled, 1)
            in_tile = ps[:, 6, 0:NT * NE].rearrange("p (t e) -> p t e", e=NE)
            totals = ps[:, 6, NT * NE:2 * NT * NE].rearrange("p (t e) -> p t e", e=NE)
            then(nc.vector.tensor_copy(run[:, 0, 8:, :], totals))
            for k, d in enumerate((1, 2, 4, 8)):
                then(nc.vector.tensor_tensor(run[:, (k + 1) % 2, 8:, :], run[:, k % 2, 8:, :], run[:, k % 2, 8 - d:8 + NT - d, :], ALU.add))
            then(nc.vector.tensor_scalar(tiles_f[:, :], run[:, 0, 7 + NT, :], float(P - 1), None, ALU.add))
            then(nc.vector.tensor_copy(tiles_i[:, :], tiles_f[:, :]))
            then(nc.vector.tensor_scalar(tiles_i[:, :], tiles_i[:, :], 7, None, ALU.logical_shift_right))
            then(nc.vector.tensor_copy(ends[:, 0, 4:], tiles_i[:, :]))
            for k, d in enumerate((1, 2, 4)):
                then(nc.vector.tensor_tensor(ends[:, (k + 1) % 2, 4:], ends[:, k % 2, 4:], ends[:, k % 2, 4 - d:4 + NE - d], ALU.add))
            then(nc.vector.tensor_tensor(slot_e[:, :, :], in_tile, run[:, 0, 7:7 + NT, :], ALU.add))
            then(nc.vector.tensor_scalar(tiles_f[:, :], ends[:, 1, 3:3 + NE], float(P), None, ALU.mult))
            then(nc.vector.tensor_tensor(slot_e[:, :, :], slot_e[:, :, :], tiles_f[:, :].unsqueeze(1).to_broadcast([P, NT, NE]), ALU.add))
            for i in range(TOP):
                last = nc.vector.tensor_tensor(hot[:, i, :, :], hot[:, i, :, :], slot_e[:, :, :], ALU.mult)
            then(last)
            then(nc.vector.tensor_reduce(slot_f[:, :, :], hot[:, :, :, :], AXX, ALU.add))
            nc.vector.tensor_copy(slot[:, :, :], slot_f[:, :, :]).then_inc(slots_ready, 1)
            then(nc.vector.tensor_tensor(owner_e[:, :, :], iota_mt[:, :].unsqueeze(2).to_broadcast([1, MT, NE - 1]),
                                         ends[0:1, 1, 4:3 + NE].unsqueeze(1).to_broadcast([1, MT, NE - 1]), ALU.is_ge))
            then(nc.vector.tensor_reduce(owner_f[:, :], owner_e[:, :, :], AXX, ALU.add))
            nc.vector.tensor_copy(owner[:, :], owner_f[:, :]).then_inc(owner_ready, 1)

            def add_shared(b):
                for i in range(2):
                    dve.wait_ge(e_filled, 2 * b + i + 1)
                    two = xs[:, QT * b + 2 * i:QT * b + 2 * i + 2, :].rearrange("p t d -> p (t d)")
                    nc.vector.tensor_tensor(two, two, ps[:, 4 + 2 * (b % 2) + i, :], ALU.add).then_inc(e_added, 1)

            for b in range(SHARED_FIRST):
                if b:
                    hidden(b)
                add_shared(b)

            def hid_rows(j, par):
                dve.wait_ge(g_ready, j + 1)
                nc.vector.tensor_tensor(hid[:, par, :], gs[:, par, :], ps[:, 2 * par + 1, :], ALU.mult).then_inc(hid_ready, 1)

            def copy_hidT(j, par):
                dve.wait_ge(hidT_filled, j + 1)
                nc.vector.tensor_copy(hidT[:, par, :, :].rearrange("p m t -> p (m t)"), ps[:, 5, :]).then_inc(hidT_ready, 1)

            hid_rows(0, 0)
            slot_steps(dve, lambda j, par, more, i: (copy_hidT(j - 1, 1 - par), hid_rows(j, par)))
            copy_hidT(MT - 1, (MT - 1) % 2)

            for b in range(SHARED_FIRST, B):
                hidden(b)
                add_shared(b)
            for t in range(NT):
                for i in range(TOP):
                    n = TOP * t + i
                    dve.wait_ge(y_gathered[n % 4], 16 * (n // 4 + 1))
                    if i:
                        dve.wait_ge(combined, n)
                    nc.vector.scalar_tensor_tensor(xs[:, t, :], yg[:, n % 4, :], gate[:, t, i:i + 1], xs[:, t, :],
                                                   ALU.mult, ALU.add).then_inc(combined, 1)

        @block.tensor
        def _(pe):
            pe.wait_ge(zeroed, 7)
            for n in range(B * DC):
                b, c = n // DC, n % DC
                pe.wait_ge(xn_ready, QT * (b + 1))
                turn(pe, xn, b, c, n, turned)
            pe.wait_ge(c_loaded, 16)
            for n in range(B * DC):
                pe.wait_ge(xnT_ready, n + 1)
                turn(pe, cs, n // DC, n % DC, n, turned)

            def await_bank(use, hp, last):
                for s, v in bank_left(use, hp, last):
                    pe.wait_ge(s, v)
                return ps[:, bank_of[use], :]

            def project(b, hp, last, first=False):
                if first:
                    pe.wait_ge(parts_ready, B * DC)
                pe.wait_ge(wqkv_loaded, 32 * (hp + (b == 0 and not first)) + 32)
                for s, filled in ((0, q_filled), (1, k_filled), (2, v_filled)):
                    use = ("qkv"[s], b, 0)
                    o = ps[:, bank_of[use], :] if first else await_bank(use, hp, last)
                    if s < 2:
                        for c in range(DC):
                            mm = nc.tensor.matmul(o, wqkv[:, c, s, :], xnT[:, c, b * S:(b + 1) * S], start=(c == 0), stop=(c == DC - 1))
                    else:
                        for t in range(QT):
                            for c in range(DC):
                                k0 = b * S + t * P
                                mm = nc.tensor.matmul(o[:, t * P:(t + 1) * P], xnT[:, c, k0:k0 + P], wqkv[:, c, 2, :],
                                                      start=(c == 0), stop=(c == DC - 1))
                    mm.then_inc(filled, 1)

            def scores(n, b):
                pe.wait_ge(q_ready, 2 * n + 2)
                pe.wait_ge(k_ready, n + 1)
                for t in range(QT):
                    if b >= 1:
                        pe.wait_ge(exp_done, 2 * QT * (n - 1) + 2 * t + 2)
                    for h in range(2):
                        o = ps[:, t, h * KW:(h + 1) * KW]
                        q = (qa, qb)[h][:, b % 2, t * P:(t + 1) * P]
                        nc.tensor.matmul(o, ident_b[:], mask[:, min(t, 1), :], start=True, stop=False)
                        mm = nc.tensor.matmul(o, q, kt[:, b % 2, t * P:t * P + KW], start=False, stop=True)
                    mm.then_inc(scores_filled, 1)

            def attend(n, b, hp, last):
                for t in range(QT):
                    use = ("pT", b, t)
                    pe.wait_ge(probs_ready, QT * n + t + 1)
                    bank = await_bank(use, hp, last)
                    for h in range(2):
                        for k in ((1,) if t == 0 else (0, 1)):
                            o = bank[:, (2 * h + k) * P:(2 * h + k + 1) * P]
                            mm = nc.tensor.transpose(o, pr[:, b % 2, t, h, k * P:(k + 1) * P], ident[:])
                    mm.then_inc(prT_filled, 1)
                pe.wait_ge(prT_ready, 7 * n + 7)
                pe.wait_ge(v_ready, n + 1)
                for t in range(QT):
                    w = KW if t < QT - 1 else P
                    for h in range(2):
                        mm = nc.tensor.matmul(ps[h * DH:(h + 1) * DH, 6, t * P:t * P + w], vv[:, b % 2, t, h * DH:(h + 1) * DH],
                                              prT[:, h, t, 0:w], start=(t == 0), stop=(t == QT - 1), skip_group_check=True)
                mm.then_inc(oT_filled, 1)

            def project_out(n, b, hp, last):
                pe.wait_ge(oT_ready, n + 1)
                pe.wait_ge(wo_loaded, 16 * hp + 16)
                for i in range(2):
                    bank = await_bank(("y", b, i), hp, last)
                    for j in range(2):
                        t = 2 * i + j
                        mm = nc.tensor.matmul(bank[:, j * D:(j + 1) * D], oT[:, t * P:(t + 1) * P], wo[:, :],
                                              start=True, stop=True)
                    mm.then_inc(y_filled, 1)

            pe.wait_ge(consts_ready, 9)
            project(0, 0, False, first=True)

            def head_pair(hp, last):
                n0 = hp * B
                for b in range(B):
                    scores(n0 + b, b)
                    if b >= 1:
                        attend(n0 + b - 1, b - 1, hp, last)
                        project_out(n0 + b - 1, b - 1, hp, last)
                    if b < B - 1 or not last:
                        project((b + 1) % B, hp, last)
                attend(n0 + B - 1, B - 1, hp, last)
                project_out(n0 + B - 1, B - 1, hp, last)

            with pe.Fori(0, HP - 1) as hp:
                head_pair(hp, False)
            head_pair(HP - 1, True)

            for n in range(B * DC):
                b, c = n // DC, n % DC
                pe.wait_ge(xn_ready, NT + QT * (b + 1))
                turn(pe, xn, b, c, n, turned)

            def cross_scores(n, g, u):
                h, q2 = u // 2, u % 2
                hh = HG * g + h
                if u >= 2 or not isinstance(n, int) or n > 0:
                    pe.wait_ge(nmax_ready, 8 * n + u - 1)
                for j in range(2):
                    mm = nc.tensor.matmul(ps[:, 2 * (u % 2) + j, :], qp[0:XS, hh, (2 * q2 + j) * P:(2 * q2 + j + 1) * P],
                                          kp[0:XS, hh, :], start=True, stop=True)
                mm.then_inc(xs_filled, 1)

            def turn_max(n, par, left=0):
                pe.wait_ge(m2_ready, n + 1)
                if left:
                    pe.wait_ge(x2_ready, left)
                for t in range(QT):
                    o = ps[0:2 * HG, 7, t * P // 2:(t + 1) * P // 2].bitcast(BF16)
                    src = xm2[:, par, :, :, t].rearrange("p i h -> p (i h)")
                    mm = nc.tensor.transpose(o, src, ident_b[:])
                mm.then_inc(m2T_filled, 1)

            def cross_exp_scores(n, g, u):
                k, h = u // HG, u % HG
                if u >= 2:
                    pe.wait_ge(ex_ready, 16 * n + u - 1)
                mm = nc.tensor.matmul(ps[:, 4 + u % 2, :], kp[0:XS + 2, HG * g + h, k * P:(k + 1) * P], qp[0:XS + 2, HG * g + h, :],
                                      start=True, stop=True)
                mm.then_inc(st_filled, 1)

            def cross_values(n, g, k):
                pe.wait_ge(ex_ready, 16 * n + 4 * k + 4)
                for h in range(HG):
                    mm = nc.tensor.matmul(ps[32 * h:32 * h + 32, 6, :], vp[:, k, HG * g + h, :], ex[:, k % 2, h, :],
                                          start=(k == 0), stop=(k == QT - 1), skip_group_check=True)
                mm.then_inc(pv_done, 1)

            pe.wait_ge(parts_ready, 2 * B * DC)
            for n in range(2):
                pe.wait_ge(split_loaded[n], 16 * 9)
                for u in range(8):
                    cross_scores(n, n, u)
            turn_max(0, 0)

            def cross_group(n, b, g, more, more_max):
                if more:
                    pe.wait_ge(split_loaded[(g + 2) % NG], 16 * 9 * (b + 1 + (g + 2) // NG))
                pe.wait_ge(m_loaded, 32 * (n + 1))
                if g == 0:
                    pe.wait_ge(vp_ready, QT * (b + 1))
                for u in range(8):
                    if more:
                        cross_scores(n + 2, (g + 2) % NG, u)
                    if u == 3 and more_max:
                        turn_max(n + 1, (g + 1) % 2, left=0 if more else n)
                    cross_exp_scores(n, g, 2 * u)
                    cross_exp_scores(n, g, 2 * u + 1)
                    if u in (3, 5, 7):
                        cross_values(n, g, (u - 3) // 2)
                cross_values(n, g, 3)
                pe.wait_ge(xoT_ready, n + 1)
                pe.wait_ge(m2T_ready, n + 2 if more_max else n + 1)
                if not more_max:
                    pe.wait_ge(x2_ready, n)
                for t in range(QT):
                    mm = nc.tensor.transpose(ps[:, 7, t * P:(t + 1) * P], xoT[:, t * P:(t + 1) * P], ident[:])
                mm.then_inc(xoN_filled, 1)

            with pe.Fori(0, B - 1) as b:
                for g in range(NG):
                    cross_group(b * NG + g, b, g, True, True)
            for g in range(NG):
                cross_group((B - 1) * NG + g, B - 1, g, g < NG - 2, g < NG - 1)

            for n in range(B * DC):
                b, c = n // DC, n % DC
                pe.wait_ge(xn_ready, 2 * NT + QT * (b + 1))
                turn(pe, xn, b, c, n, turned)
            pe.wait_ge(wr_loaded, 16)
            pe.wait_ge(xnT_ready, 2 * B * DC)
            for t in range(NT):
                for c in range(DC):
                    mm = nc.tensor.matmul(ps[:, 7, t * NE:(t + 1) * NE], xnT[:, c, t * P:(t + 1) * P], wr[:, c, :],
                                          start=(c == 0), stop=(c == DC - 1))
            mm.then_inc(logits_filled, 1)

            def shared_hidden(b):
                for m in range(FC):
                    u = b * FC + m
                    if u >= 2:
                        pe.wait_ge(h_ready, u - 1)
                    for w, bank in ((wa, 2 * (m % 2)), (wb, 2 * (m % 2) + 1)):
                        for c in range(DC):
                            mm = nc.tensor.matmul(ps[:, bank, :], w[:, c, m * P:(m + 1) * P], xnT[:, c, b * S:(b + 1) * S],
                                                  start=(c == 0), stop=(c == DC - 1))
                    mm.then_inc(h_filled, 1)

            def shared_out(b):
                pe.wait_ge(h_ready, (b + 1) * FC)
                if b >= 2:
                    pe.wait_ge(e_added, 2 * b - 2)
                for i in range(2):
                    for j in range(2):
                        t = 2 * i + j
                        for m in range(FC):
                            mm = nc.tensor.matmul(ps[:, 4 + 2 * (b % 2) + i, j * D:(j + 1) * D], ht[:, b % 2, m, t * P:(t + 1) * P],
                                                  wc[:, m, :], start=(m == 0), stop=(m == FC - 1))
                    mm.then_inc(e_filled, 1)

            pe.wait_ge(shared_loaded, 48)
            for b in range(SHARED_FIRST):
                shared_hidden(b)
                if b == 0:
                    pe.wait_ge(sel_ready, 1)
                    pe.wait_ge(consts_ready, 14)
                    chosen = sel[:, :, :].rearrange("p t e -> p (t e)")
                    nc.tensor.matmul(ps[:, 6, 0:P], before[:], chosen, start=True, stop=True)
                    nc.tensor.matmul(ps[:, 6, P:2 * P], ones[:], chosen, start=True, stop=True).then_inc(counts_filled, 1)
                if b == 1:
                    pe.wait_ge(slots_ready, 1)
                shared_out(b)

            def turn_rows(j, par, loads):
                pe.wait_ge(rows_loaded[par], 16 * loads)
                for c in range(DC):
                    mm = nc.tensor.transpose(ps[:, 4, c * P:(c + 1) * P], xg[:, par, c * P:(c + 1) * P], ident[:])
                mm.then_inc(rowsT_filled, 1)

            def rows_hidden(j, par):
                e = pe.value_load(owner[0:1, bass.ds(j, 1)], min_val=0, max_val=NE - 1)
                pe.wait_ge(rowsT_ready, j + 1)
                for w, bank in ((w1s, 2 * par), (w3s, 2 * par + 1)):
                    we = w[:, bass.ds(e, 1), :].rearrange("p e (c f) -> p (e c) f", c=DC)
                    for c in range(DC):
                        mm = nc.tensor.matmul(ps[:, bank, :], xgT[:, par, c, :], we[:, c, :], start=(c == 0), stop=(c == DC - 1))
                mm.then_inc(g13_filled, 1)

            def turn_hid(j, par):
                pe.wait_ge(hid_ready, j + 1)
                for m in range(FC):
                    mm = nc.tensor.transpose(ps[:, 5, m * P:(m + 1) * P], hid[:, par, m * P:(m + 1) * P], ident[:])
                mm.then_inc(hidT_filled, 1)

            def rows_out(j, par):
                e = pe.value_load(owner[0:1, bass.ds(j, 1)], min_val=0, max_val=NE - 1)
                pe.wait_ge(hidT_ready, j + 1)
                we = w2s[:, bass.ds(e, 1), :].rearrange("p e (m d) -> p (e m) d", m=FC)
                for m in range(FC):
                    mm = nc.tensor.matmul(ps[:, 6 + par, 0:D], hidT[:, par, m, :], we[:, m, :], start=(m == 0), stop=(m == FC - 1))
                mm.then_inc(yrow_filled, 1)

            pe.wait_ge(owner_ready, 1)
            pe.wait_ge(w13_loaded, 16 * 2 * NE)
            pe.wait_ge(w2_loaded, 16 * NE)
            pe.wait_ge(e_added, 2 * SHARED_FIRST)
            turn_rows(0, 0, 1)
            pe.wait_ge(rowsT_ready, 1)
            turn_rows(1, 1, 1)
            rows_hidden(0, 0)

            def slot_step(j, par, more, i):
                if more:
                    pe.wait_ge(rowsT_ready, j + 1)
                    turn_rows(j + 1, 1 - par, i + 2)
                turn_hid(j - 1, 1 - par)
                rows_hidden(j, par)
                rows_out(j - 1, 1 - par)

            slot_steps(pe, slot_step)
            turn_hid(MT - 1, (MT - 1) % 2)
            rows_out(MT - 1, (MT - 1) % 2)
            pe.wait_ge(yrow_ready, MT)
            for b in range(SHARED_FIRST, B):
                shared_hidden(b)
                shared_out(b)


_INS = ["x", "ctx_1024", "L0_attn_w_qkv", "L0_attn_w_out", "L0_ffn_w_router", "L0_ffn_w1", "L0_ffn_w3", "L0_ffn_w2",
        "L0_ffn_sw1", "L0_ffn_sw3", "L0_ffn_sw2"]
_OUTS = [((4, 512, 256), "float32")]


def kernel(**inputs):
    import numpy as _np
    import concourse.bacc as _bacc
    from concourse import mybir as _mybir
    from concourse.bass_utils import run_bass_kernel_spmd as _run

    nc = _bacc.Bacc("TRN2", target_bir_lowering=False, num_devices=1)
    arrays, args = {}, []
    for name in _INS:
        a = _np.ascontiguousarray(inputs[name])
        arrays[f"in_{name}_dram"] = a
        args.append(nc.dram_tensor(f"in_{name}_dram", a.shape, _mybir.dt.from_np(a.dtype), kind="ExternalInput").ap())
    for i, (shape, dtype) in enumerate(_OUTS):
        dt = _mybir.dt.from_np(_np.dtype(dtype))
        args.append(nc.dram_tensor(f"out_{i}_dram", shape, dt, kind="ExternalOutput").ap())
    decoder_layer(nc, *args)
    r = _run(nc, [arrays], core_ids=[0])
    return r.results[0]["out_0_dram"]
```

```python
from contextlib import ExitStack

import concourse.bass as bass
import concourse.mybir as mybir
from concourse.alu_op_type import AluOpType as ALU

F32 = mybir.dt.float32
BF16 = mybir.dt.bfloat16
U32 = mybir.dt.uint32
I32 = mybir.dt.int32
ACT = mybir.ActivationFunctionType
AXX = mybir.AxisListType.X

P = 128
B, S, D = 4, 512, 256
T = B * S
NT = T // P
QT = S // P
DC = D // P
H = 16
DH = 64
HP = H * DH // P
W = 64
KW = W + P
XD = D // H
XS = 6 * XD
HG = 4
NG = H // HG
NE = 8
F = 512
FC = F // P
TOP = 2
MT = (TOP * T + NE * (P - 1)) // P
assert MT % 2 == 1
SLOTS = MT * P
PARTS = 4
SHARED_PIECES = 3
SHARED_FIRST = 2
EPS = 1e-5
ROOTS_AT, EXP_AT = 10, 15
AHEAD = 17
UNITS = 8 * B * NG
MASKED = -3.0e38


def decoder_layer(nc, x, ctx, w_qkv, w_out, w_router, w1, w3, w2, sw1, sw3, sw2, out):
    with ExitStack() as es:
        def sb(name, shape, dt=F32):
            return es.enter_context(nc.sbuf_tensor(name, shape, dt))

        def sem(name):
            return es.enter_context(nc.semaphore(name))

        ps = es.enter_context(nc.psum_tensor("ps", [P, 8, 512], F32))

        xs = sb("xs", [P, NT, D])
        xn = sb("xn", [P, NT, D])
        xnT = sb("xnT", [P, DC, T])
        stats = sb("stats", [P, NT, 6])
        mv = sb("mv", [P, NT, 2])
        std = sb("std", [P, NT])
        rstd = sb("rstd", [P, NT])
        ident = sb("ident", [P, P])
        ident_b = sb("ident_b", [P, P], BF16)
        mask = sb("mask", [P, 2, KW], BF16)

        WREG = NE * DC * F
        region_a = sb("region_a", [P, 2 * WREG])
        region_b = sb("region_b", [P, 19200])

        def planner(region):
            at = [0]

            def view(*shape, dt=F32):
                n = 1
                for k in shape:
                    n *= k
                words = n if dt is F32 else n // 2
                ap = region[:, at[0]:at[0] + words]
                at[0] += words
                assert at[0] <= region.shape[1], (at[0], region.shape)
                ap = ap if dt is F32 else ap.bitcast(dt)
                names = "abcd"[:len(shape)]
                return ap.rearrange(f"p ({' '.join(names)}) -> p {' '.join(names)}", **dict(zip(names[1:], shape[1:])))
            return view

        view = planner(region_a)
        wqkv = view(DC, 3, P)
        wo = view(D)
        qa = view(2, S)
        qb = view(2, S)
        kt = view(2, W + S)
        vv = view(2, QT, P)
        pr = region_a[:, 8192:8192 + 4096].rearrange("p (i t h k) -> p i t h k", i=2, t=QT, h=2)
        prT = view(2, QT, KW)
        oT = view(S)
        nmax = sb("nmax", [P, 2, 2 * QT])
        rsum = sb("rsum", [P, 2, 2 * QT])
        rinv = sb("rinv", [P, 2, 2 * QT])

        view = planner(region_b)
        cs = view(NT, D)
        qp = view(H, S, dt=BF16)
        ctxT = region_b[:, NT * D:2 * NT * D].rearrange("p (n s) -> p n s", s=S)
        kp = view(H, S, dt=BF16)
        vp = view(QT, H, 32)
        view_split = planner(region_b)
        view_split(3 * NT * D + 2048)
        part = view_split(PARTS, 3, S, dt=BF16)
        rest = view_split(2, S)
        ex = view(2, HG, S)
        xoT = view(S)
        xnm = sb("xnm", [P, 2, HG, QT])
        xm2 = sb("xm2", [P, 2, 2, HG, QT], BF16)
        xmT = sb("xmT", [2 * HG, S], BF16)
        xr = sb("xr", [P, QT, HG])
        xo = sb("xo", [P, QT, HG, XD])

        view = planner(region_a)
        w1s = view(NE, DC * F)
        w3s = view(NE, DC * F)
        view = planner(region_b)
        wa = view(DC, F)
        wb = view(DC, F)
        wc = view(FC, D)
        w2s = view(NE, FC * D)
        gt = view(2, S)
        ht = view(2, FC, S)
        xg, xgT = xn[:, 0:2, :], xn[:, 2:4, :].rearrange("p i (c t) -> p i c t", c=DC)
        yrow = xn[:, 4:6, :]
        yg = region_a[:, 0:TOP * NT * D].rearrange("p (n d) -> p n d", d=D)
        gs = gt
        hid = view(2, F)
        hidT = view(2, FC, P)
        wr = sb("wr", [P, DC, NE])
        lmax = sb("lmax", [P, NT])
        lg = sb("lg", [P, NT, NE])
        top = sb("top", [P, NT, 8])
        tix = sb("tix", [P, NT, 8], U32)
        tixf = sb("tixf", [P, NT, TOP])
        gsum = sb("gsum", [P, NT])
        gate = sb("gate", [P, NT, TOP])
        iota8 = sb("iota8", [P, NE])
        iota_mt = sb("iota_mt", [1, MT])
        hot = sb("hot", [P, TOP, NT, NE])
        sel = sb("sel", [P, NT, NE])
        before = sb("before", [P, P])
        ones = sb("ones", [P, P])
        run = sb("run", [P, 2, 8 + NT, NE])
        tiles_f = sb("tiles_f", [P, NE])
        tiles_i = sb("tiles_i", [P, NE], I32)
        ends = sb("ends", [P, 2, 4 + NE])
        slot_e = sb("slot_e", [P, NT, NE])
        slot_f = sb("slot_f", [P, TOP, NT])
        slot = sb("slot", [P, TOP, NT], U32)
        owner_e = sb("owner_e", [1, MT, NE - 1])
        owner_f = sb("owner_f", [1, MT])
        owner = sb("owner", [1, MT], I32)
        zrow = sb("zrow", [P, D])

        xsort = nc.dram_tensor("xsort", (SLOTS, D), F32, kind="Internal").ap()
        ysort = nc.dram_tensor("ysort", (SLOTS, D), F32, kind="Internal").ap()
        scr_q = nc.dram_tensor("scr_q", (H, 3, XD, T), BF16, kind="Internal").ap()
        scr_k = nc.dram_tensor("scr_k", (H, 3, XD, T), BF16, kind="Internal").ap()

        x_loaded = [sem(f"x_loaded{b}") for b in range(B)]
        c_loaded = sem("c_loaded")
        stats_ready, mv_ready, var_ready, std_ready = sem("stats_ready"), sem("mv_ready"), sem("var_ready"), sem("std_ready")
        rstd_ready, xn_ready = sem("rstd_ready"), sem("xn_ready")
        turned, xnT_ready = sem("turned"), sem("xnT_ready")
        ident_zeroed, ident_ready, zeros_ready = sem("ident_zeroed"), sem("ident_ready"), sem("zeros_ready")
        mask_zeroed, mask_cut, masks_ready = sem("mask_zeroed"), sem("mask_cut"), sem("masks_ready")
        cross_zeroed, cross_consts_ready = sem("cross_zeroed"), sem("cross_consts_ready")
        before_filled, route_consts_ready, zrow_ready = sem("before_filled"), sem("route_consts_ready"), sem("zrow_ready")
        ctx_turned, ctxT_ready, xn3T_ready = sem("ctx_turned"), sem("ctxT_ready"), sem("xn3T_ready")
        ctx_hi, ctx_rest1, ctx_mid, ctx_parts_ready = sem("ctx_hi"), sem("ctx_rest1"), sem("ctx_mid"), sem("ctx_parts_ready")
        hi_ready, rest1_ready, mid_ready, parts_ready = sem("hi_ready"), sem("rest1_ready"), sem("mid_ready"), sem("parts_ready")
        parts_stored = [sem(f"parts_stored{i}") for i in range(PARTS)]

        wqkv_loaded, wo_loaded = sem("wqkv_loaded"), sem("wo_loaded")
        q_filled, k_filled, v_filled = sem("q_filled"), sem("k_filled"), sem("v_filled")
        q_ready, k_ready, v_ready = sem("q_ready"), sem("k_ready"), sem("v_ready")
        scores_filled, max_ready, exp_done = sem("scores_filled"), sem("max_ready"), sem("exp_done")
        masked, rinv_ready, probs_ready = sem("masked"), sem("rinv_ready"), sem("probs_ready")
        prT_filled, prT_ready = sem("prT_filled"), sem("prT_ready")
        oT_filled, oT_ready, y_filled = sem("oT_filled"), sem("oT_ready"), sem("y_filled")
        x1_ready = sem("x1_ready")

        split_loaded = [sem(f"split_loaded{g}") for g in range(NG)]
        vp_ready = sem("vp_ready")
        xs_filled = sem("xs_filled")
        nmax_ready, part1_ready, m2_ready = sem("nmax_ready"), sem("part1_ready"), sem("m2_ready")
        m2T_filled, m2T_ready, m_loaded = sem("m2T_filled"), sem("m2T_ready"), sem("m_loaded")
        st_filled, ex_ready, pv_done = sem("st_filled"), sem("ex_ready"), sem("pv_done")
        xoT_ready, xoN_filled, xr_ready, xo_ready, x2_ready = sem("xoT_ready"), sem("xoN_filled"), sem("xr_ready"), sem("xo_ready"), sem("x2_ready")

        wr_loaded, logits_filled, route = sem("wr_loaded"), sem("logits_filled"), sem("route")
        e_ready, exp_e_ready, counts_filled, sel_ready = sem("e_ready"), sem("exp_e_ready"), sem("counts_filled"), sem("sel_ready")
        owner_ready, slots_ready, xsort_zeroed, xsorted = sem("owner_ready"), sem("slots_ready"), sem("xsort_zeroed"), sem("xsorted")
        w13_loaded, w2_loaded, shared_loaded = sem("w13_loaded"), sem("w2_loaded"), sem("shared_loaded")
        h_filled, silu_ready, h_ready = sem("h_filled"), sem("silu_ready"), sem("h_ready")
        e_filled, e_added, x3_stored = sem("e_filled"), sem("e_added"), sem("x3_stored")
        rows_loaded = [sem("rows_loaded0"), sem("rows_loaded1")]
        rowsT_filled, rowsT_ready, g13_filled, g_ready = sem("rowsT_filled"), sem("rowsT_ready"), sem("g13_filled"), sem("g_ready")
        hid_ready, hidT_filled, hidT_ready, yrow_filled, yrow_ready = sem("hid_ready"), sem("hidT_filled"), sem("hidT_ready"), sem("yrow_filled"), sem("yrow_ready")
        y_stored = [sem("y_stored0"), sem("y_stored1")]
        y_gathered = [sem(f"y_gathered{t}") for t in range(NT)]
        combined0, combined = sem("combined0"), sem("combined")

        x_in = x.rearrange("b (t p) d -> b p t d", p=P)
        c_in = ctx.rearrange("b (t p) d -> p (b t) d", p=P)
        y_out = out.rearrange("b (t p) d -> b p t d", p=P)
        wqkv_in = w_qkv.rearrange("(c p) (s h n) -> c p s h n", p=P, s=3, h=HP)
        wo_in = w_out.rearrange("(h p) n -> h p n", p=P)

        w1_in, w3_in = (w.rearrange("e (c p) f -> e p c f", p=P) for w in (w1, w3))
        w2_in = w2.rearrange("e (c p) d -> p e c d", p=P)
        xsort_t, ysort_t = (r.rearrange("(j p) d -> j p d", p=P) for r in (xsort, ysort))
        sw1_in, sw3_in, sw2_in = (w.rearrange("(c p) f -> p c f", p=P) for w in (sw1, sw3, sw2))

        def ln_stats(dve, n, t0, t1):
            for t in range(t0, t1):
                nc.vector.bn_stats(stats[:, t, :], xs[:, t, :]).then_inc(stats_ready, 1)
            dve.wait_ge(stats_ready, NT * n + t1)
            for t in range(t0, t1):
                nc.vector.bn_aggr(mv[:, t, :], stats[:, t, :]).then_inc(mv_ready, 1)
            dve.wait_ge(mv_ready, NT * n + t1)
            nc.vector.tensor_scalar(rstd[:, t0:t1], mv[:, t0:t1, 1], EPS, None, ALU.add).then_inc(var_ready, 1)

        def ln_rows(dve, n, t0, t1, k):
            dve.wait_ge(std_ready, k)
            nc.vector.reciprocal(rstd[:, t0:t1], std[:, t0:t1]).then_inc(rstd_ready, 1)
            dve.wait_ge(rstd_ready, k)
            for t in range(t0, t1):
                nc.vector.tensor_scalar(xn[:, t, :], xs[:, t, :], mv[:, t, 0:1], rstd[:, t:t + 1],
                                        ALU.subtract, ALU.mult).then_inc(xn_ready, 1)

        def ln_scalar(act, t0, t1, k):
            act.wait_ge(var_ready, k)
            nc.scalar.activation(std[:, t0:t1], rstd[:, t0:t1], ACT.Sqrt).then_inc(std_ready, 1)

        def turn(pe, src, b, c, bank, done):
            for t in range(QT):
                mm = nc.tensor.transpose(ps[:, bank, t * P:(t + 1) * P], src[:, QT * b + t, c * P:(c + 1) * P], ident[:])
            mm.then_inc(done, 1)

        def pair_steps(eng, step, finish):
            def pair(hp, first=False, last=False):
                for b in range(B):
                    step(hp, b, not (first and b == 0), not (last and b == B - 1), first, last)

            pair(0, first=True)
            with eng.Fori(1, HP - 1) as hp:
                pair(hp)
            pair(HP - 1, last=True)
            finish(HP * B - 1, B - 1)

        BANK = {("pT", 0): 4, ("pT", 1): 5, ("pT", 2): 7, ("pT", 3): 4, ("q", 0): 5, ("k", 0): 7,
                ("y", 0): 4, ("v", 0): 5, ("y", 1): 7}
        QBANK = (0, 1, 2, 3, 5, 6, 4, 7)
        XBANK = (0, 1, 2, 0, 1, 2, 4, 5)

        def slot_steps(eng, step):
            def two(i, last=False):
                step(2 * i + 1, 1, True, i)
                step(2 * i + 2, 0, not last, i)

            two(0)
            with eng.Fori(1, MT // 2 - 1) as i:
                two(i)
            two(MT // 2 - 1, last=True)

        block = es.enter_context(nc.Block())

        @block.sync
        def _(sp):
            for b in range(B):
                sp.dma_start(xs[:, QT * b:QT * (b + 1), :], x_in[b]).then_inc(x_loaded[b], 16)
            for c in range(DC):
                sp.dma_start(wqkv[:, c, :, :], wqkv_in[c, :, :, 0, :]).then_inc(wqkv_loaded, 16)
            sp.dma_start(wo[:, :], wo_in[0]).then_inc(wo_loaded, 16)
            sp.dma_start(cs[:, :, :], c_in).then_inc(c_loaded, 16)

            def store_parts(scr, ready, k0, b):
                for c in range(DC):
                    k = k0 + DC * b + c
                    sp.wait_ge(ready, k - k0 + 1)
                    for i in range(3):
                        sp.dma_start(scr[c * 8:(c + 1) * 8, i, :, b * S:(b + 1) * S], part[:, k % PARTS, i, :]).then_inc(parts_stored[k % PARTS], 16)

            def wait_stored(chunks):
                for i in range(PARTS):
                    sp.wait_ge(parts_stored[i], 48 * ((chunks + PARTS - 1 - i) // PARTS))

            def load_wqkv(hp):
                sp.wait_ge(v_filled, hp * B)
                for c in range(DC):
                    sp.dma_start(wqkv[:, c, :, :], wqkv_in[c, :, :, hp, :]).then_inc(wqkv_loaded, 16)

            def load_wo(hp):
                sp.wait_ge(y_filled, hp * 2 * B)
                sp.dma_start(wo[:, :], wo_in[hp]).then_inc(wo_loaded, 16)

            def load_keys(b, g):
                hs = slice(HG * g, HG * (g + 1))
                for seg, i in enumerate((0, 0, 0, 1, 1, 2)):
                    src = scr_k[hs, i, :, bass.ds(b * S, S)].rearrange("h d t -> d h t")
                    sp.dma_start(kp[XD * seg:XD * (seg + 1), hs, :], src).then_inc(split_loaded[g], 16)

            def load_queries(b, g):
                hs = slice(HG * g, HG * (g + 1))
                for rows, parts in ((0, 3), (3 * XD, 2), (5 * XD, 1)):
                    n = XD * parts
                    src = scr_q.rearrange("h i d t -> (i d) h t")[0:n, hs, bass.ds(b * S, S)]
                    sp.dma_start(qp[rows:rows + n, hs, :], src).then_inc(split_loaded[g], 16)

            sp.wait_ge(zrow_ready, 1)
            sp.dma_start(xsort.rearrange("(j p) d -> p j d", p=P),
                         zrow[:, :].unsqueeze(1).to_broadcast([P, MT, D])).then_inc(xsort_zeroed, 16)
            for b in range(B - 2):
                store_parts(scr_k, ctx_parts_ready, 0, b)
            load_wqkv(1)
            for b in range(B - 2, B):
                store_parts(scr_k, ctx_parts_ready, 0, b)
            load_wo(1)
            wait_stored(B * DC)
            for g in range(NG):
                load_keys(0, g)

            with sp.Fori(2, HP) as hp:
                load_wqkv(hp)
                load_wo(hp)

            for b in range(2):
                store_parts(scr_q, parts_ready, B * DC, b)
            for i in range(DC):
                sp.wait_ge(parts_stored[i], 48 * (B * DC // PARTS + 1))
            for g in range(NG):
                load_queries(0, g)
            for b in range(2, B):
                store_parts(scr_q, parts_ready, B * DC, b)

            def load_max(n, g):
                sp.wait_ge(m2T_ready, n + 1)
                for i in range(2):
                    sp.dma_start(qp[XS + i:XS + i + 1, HG * g:HG * (g + 1), :], xmT[HG * i:HG * (i + 1), :]).then_inc(m_loaded, 16)

            def load_w13(e, which):
                dst, src = ((w1s, w1_in), (w3s, w3_in))[which]
                sp.dma_start(dst[:, bass.ds(e, 1), :].rearrange("p e (c f) -> p (e c) f", c=DC), src[e]).then_inc(w13_loaded, 16)

            load_max(0, 0)
            wait_stored(2 * B * DC)
            with sp.Fori(0, B - 1) as b:
                for g in range(NG):
                    n = b * NG + g
                    load_max(n + 1, (g + 1) % NG)
                    sp.wait_ge(st_filled, 16 * (n + 1))
                    load_queries(b + 1, g)
                    load_keys(b + 1, g)
                    load_w13(2 * b + g // 2, g % 2)
            for g in range(NG - 1):
                load_max((B - 1) * NG + g + 1, g + 1)

            for e in range(2 * (B - 1), NE):
                for which in range(2):
                    load_w13(e, which)
            sp.dma_start(wr[:, :, :], w_router.rearrange("(c p) e -> p c e", p=P)).then_inc(wr_loaded, 16)
            sp.wait_ge(vp_ready, QT * B)
            for dst, src in ((wa, sw1_in), (wb, sw3_in), (wc, sw2_in)):
                sp.dma_start(dst, src).then_inc(shared_loaded, 16)
            sp.wait_ge(x2_ready, B * NG)
            for e in range(NE):
                sp.dma_start(w2s[:, e, :].rearrange("p (c d) -> p c d", c=FC), w2_in[:, e]).then_inc(w2_loaded, 16)

            def load_rows(j, par):
                sp.dma_start(xg[:, par, :], xsort_t[j]).then_inc(rows_loaded[par], 16)

            def store_rows(j, par):
                sp.wait_ge(yrow_ready, j + 1)
                sp.dma_start(ysort_t[j], yrow[:, par, :]).then_inc(y_stored[par], 16)

            sp.wait_ge(xsorted, 16 * TOP * NT)
            load_rows(0, 0)
            load_rows(1, 1)
            sp.wait_ge(rowsT_filled, 1)
            load_rows(2, 0)
            with sp.Fori(0, (MT - 3) // 2) as i:
                for k in range(2):
                    j = 2 * i + k
                    sp.wait_ge(rowsT_filled, j + 2)
                    load_rows(j + 3, (k + 1) % 2)
                    store_rows(j, k)
            for j in range(MT - 3, MT):
                store_rows(j, j % 2)
            for b in range(B):
                sp.wait_ge(combined, QT * (b + 1))
                sp.dma_start(y_out[b], xs[:, QT * b:QT * (b + 1), :]).then_inc(x3_stored, 16)
            sp.wait_ge(x3_stored, 16 * B)

        @block.gpsimd
        def _(pool):
            nc.gpsimd.memset(ident[:], 0.0).then_inc(ident_zeroed, 1)
            nc.gpsimd.memset(mask[:], 0.0).then_inc(mask_zeroed, 1)
            pool.wait_ge(ident_zeroed, 1)
            nc.gpsimd.affine_select(out=ident[:], in_=ident[:], compare_op=ALU.not_equal, fill=1.0, base=0,
                                    pattern=[[-1, P]], channel_multiplier=1).then_inc(ident_ready, 1)
            for buf in (qa[:], qb[:], kt[:, :, 0:W], pr[:, :, :, :, 0:W]):
                nc.gpsimd.memset(buf, 0.0).then_inc(zeros_ready, 1)
            pool.wait_ge(ident_ready, 1)
            nc.gpsimd.tensor_copy(ident_b[:], ident[:]).then_inc(masks_ready, 1)
            pool.wait_ge(mask_zeroed, 1)
            for v in range(2):
                nc.gpsimd.affine_select(out=mask[:, v, :], in_=mask[:, v, :], compare_op=ALU.is_ge, fill=MASKED,
                                        base=W, pattern=[[-1, KW]], channel_multiplier=1).then_inc(mask_cut, 1)
            pool.wait_ge(mask_cut, 2)
            for v in range(2):
                nc.gpsimd.affine_select(out=mask[:, v, :], in_=mask[:, v, :], compare_op=ALU.is_ge, fill=MASKED,
                                        base=-1, pattern=[[1, KW]], channel_multiplier=-1).then_inc(mask_cut, 1)
            pool.wait_ge(mask_cut, 4)
            nc.gpsimd.memset(mask[:, 0, 0:W], MASKED).then_inc(masks_ready, 1)
            nc.gpsimd.memset(zrow[:], 0.0).then_inc(zrow_ready, 1)
            nc.gpsimd.memset(vp[:], 0.0).then_inc(cross_zeroed, 1)
            pool.wait_ge(cross_zeroed, 1)
            nc.gpsimd.memset(kp[XS:XS + 2, :, :], 1.0).then_inc(cross_consts_ready, 1)
            pool.wait_ge(cross_consts_ready, 1)
            nc.gpsimd.memset(vp[:, :, :, XD:XD + 1], 1.0).then_inc(cross_consts_ready, 1)
            nc.gpsimd.iota(iota8[:], [[1, NE]], base=0, channel_multiplier=0,
                           allow_small_or_imprecise_dtypes=True).then_inc(route_consts_ready, 1)
            nc.gpsimd.memset(before[:], 1.0).then_inc(before_filled, 1)
            nc.gpsimd.memset(ones[:], 1.0).then_inc(route_consts_ready, 1)
            nc.gpsimd.memset(run[:], 0.0).then_inc(route_consts_ready, 1)
            nc.gpsimd.memset(ends[:], 0.0).then_inc(route_consts_ready, 1)
            nc.gpsimd.iota(iota_mt[:], [[1, MT]], base=0, channel_multiplier=0,
                           allow_small_or_imprecise_dtypes=True).then_inc(route_consts_ready, 1)
            pool.wait_ge(before_filled, 1)
            nc.gpsimd.affine_select(out=before[:], in_=before[:], compare_op=ALU.is_gt, fill=0.0, base=0,
                                    pattern=[[1, P]], channel_multiplier=-1).then_inc(route_consts_ready, 1)

            def values(b):
                src = cs[:, bass.ds(b * QT, QT), :].rearrange("p t (h d) -> p t h d", h=H)
                for t in range(QT):
                    nc.gpsimd.tensor_copy(vp[:, t, :, 0:XD], src[:, t]).then_inc(vp_ready, 1)

            pool.wait_ge(c_loaded, 16)
            pool.wait_ge(cross_consts_ready, 2)
            values(0)

            with pool.Fori(0, HP) as hp:
                for b in range(B):
                    n = hp * B + b
                    for t in range(QT):
                        if t % 2 == 0:
                            pool.wait_ge(rinv_ready, 2 * n + t // 2 + 1)
                        cur = pr[:, b % 2, t, :, W:]
                        inv = rinv[:, b % 2, 2 * t:2 * t + 2].unsqueeze(2).to_broadcast([P, 2, KW])
                        nc.gpsimd.tensor_tensor(cur, cur, inv, ALU.mult).then_inc(probs_ready, 1)

            for m in range(B * DC):
                pool.wait_ge(mid_ready, m + 1)
                nc.gpsimd.tensor_tensor(part[:, m % PARTS, 2, :], rest[:, m % 2, :], part[:, m % PARTS, 1, :],
                                        ALU.subtract).then_inc(parts_ready, 1)

            with pool.Fori(1, B) as b:
                pool.wait_ge(pv_done, NG * QT * b)
                values(b)

            pool.wait_ge(slots_ready, 1)
            pool.wait_ge(xsort_zeroed, 16)
            pool.wait_ge(xn_ready, 3 * NT)
            for t in range(NT):
                for i in range(TOP):
                    nc.gpsimd.indirect_dma_start(out=xsort, out_offset=bass.IndirectOffsetOnAxis(ap=slot[:, i, t:t + 1], axis=0),
                                                 in_=xn[:, t, :], in_offset=None).then_inc(xsorted, 16)
            pool.wait_ge(y_stored[0], 16 * ((MT + 1) // 2))
            pool.wait_ge(y_stored[1], 16 * (MT // 2))
            for t in range(NT):
                for i in range(TOP):
                    n = TOP * t + i
                    nc.gpsimd.indirect_dma_start(out=yg[:, n, :], out_offset=None, in_=ysort,
                                                 in_offset=bass.IndirectOffsetOnAxis(ap=slot[:, i, t:t + 1], axis=0)).then_inc(y_gathered[t], 16)

        @block.scalar
        def _(act):
            def copy_xnT(b):
                for c in range(DC):
                    n = DC * b + c
                    act.wait_ge(turned, n + 1)
                    nc.scalar.activation(xnT[:, c, b * S:(b + 1) * S], ps[:, n % 4, :], ACT.Copy).then_inc(xnT_ready, 1)

            def split_hi(b):
                for c in range(DC):
                    m = DC * b + c
                    k = B * DC + m
                    act.wait_ge(turned, k + 1)
                    act.wait_ge(parts_stored[k % PARTS], 48 * (k // PARTS))
                    nc.scalar.activation(part[:, k % PARTS, 0, :], ps[:, QBANK[m], :], ACT.Copy, scale=XD ** -0.5).then_inc(hi_ready, 1)
            def split_mid(b):
                for c in range(DC):
                    m = DC * b + c
                    k = B * DC + m
                    act.wait_ge(rest1_ready, m + 1)
                    nc.scalar.activation(part[:, k % PARTS, 1, :], rest[:, m % 2, :], ACT.Copy).then_inc(mid_ready, 1)

            def exp_scores(n, b):
                for t in range(QT):
                    if t % 2 == 0:
                        act.wait_ge(max_ready, 2 * n + t // 2 + 1)
                    for h in range(2):
                        j = 2 * t + h
                        nc.scalar.activation(pr[:, b % 2, t, h, W:], ps[:, t, h * KW:(h + 1) * KW], ACT.Exp,
                                             bias=nmax[:, b % 2, j:j + 1],
                                             accum_out=rsum[:, b % 2, j:j + 1]).then_inc(exp_done, 1)

            def copy_q(n, b):
                act.wait_ge(q_filled, n + 1)
                bank = BANK["q", 0]
                nc.scalar.activation(qa[0:DH, b % 2, :], ps[0:DH, bank, :], ACT.Copy, scale=DH ** -0.5).then_inc(q_ready, 1)
                nc.scalar.activation(qb[DH:P, b % 2, :], ps[DH:P, bank, :], ACT.Copy, scale=DH ** -0.5).then_inc(q_ready, 1)

            def copy_oT(n):
                act.wait_ge(oT_filled, n + 1)
                nc.scalar.activation(oT[:, :], ps[:, 6, :], ACT.Copy).then_inc(oT_ready, 1)

            def copy_ctxT(m):
                act.wait_ge(ctx_turned, m + 1)
                nc.scalar.activation(ctxT[:, m, :], ps[:, 6, :], ACT.Copy).then_inc(ctxT_ready, 1)

            for b in range(B):
                ln_scalar(act, QT * b, QT * (b + 1), b + 1)
                if b >= 1:
                    copy_xnT(b - 1)
                if b == 2:
                    act.wait_ge(zeros_ready, 4)
                    copy_q(0, 0)
            copy_xnT(B - 1)

            def pair_step(hp, b, prior, more, first, last):
                n = hp * B + b
                if first:
                    copy_ctxT(DC * b)
                if more:
                    copy_q(n + 1, (b + 1) % B)
                if prior:
                    copy_oT(n - 1)
                exp_scores(n, b)
                if first:
                    copy_ctxT(DC * b + 1)
                if last and b >= 2:
                    ln_scalar(act, QT * (b - 2), QT * (b - 1), B + b - 1)

            def pair_finish(n, b):
                split_hi(0)
                split_mid(0)
                split_hi(1)
                ln_scalar(act, 2 * QT, 3 * QT, B + 3)
                split_mid(1)
                copy_oT(n)
                split_hi(2)
                ln_scalar(act, 3 * QT, 4 * QT, B + 4)
                split_mid(2)
                split_hi(3)
                split_mid(3)

            pair_steps(act, pair_step, pair_finish)

            def copy_mT(n):
                act.wait_ge(m2T_filled, n + 1)
                if not isinstance(n, int) or n >= 1:
                    act.wait_ge(m_loaded, 32 * n)
                nc.scalar.activation(xmT[:, :], ps[0:2 * HG, 7, 0:S // 2].bitcast(BF16), ACT.Copy).then_inc(m2T_ready, 1)

            copy_mT(0)

            for i in range(PARTS):
                act.wait_ge(parts_stored[i], 48 * (2 * B * DC // PARTS))

            def exp_logits(k, t0, t1):
                act.wait_ge(e_ready, k + 1)
                nc.scalar.activation(lg[:, t0:t1, :], lg[:, t0:t1, :], ACT.Exp).then_inc(exp_e_ready, 1)

            def exponentials(n, u):
                k, h = u // HG, u % HG
                act.wait_ge(st_filled, 16 * n + u + 1)
                if k >= 2:
                    act.wait_ge(pv_done, 4 * n + k - 1)
                nc.scalar.activation(ex[:, k % 2, h, :], ps[:, 4 + u % 2, :], ACT.Exp).then_inc(ex_ready, 1)

            exponentials(0, 0)

            def cross_group(n, more, at=None):
                for u in range(1, 16):
                    if at and u == at[0]:
                        at[1]()
                    exponentials(n, u)
                    if u == 9 and more:
                        copy_mT(n + 1)
                if more:
                    act.wait_ge(pv_done, 4 * n + 3)
                    exponentials(n + 1, 0)
                act.wait_ge(pv_done, 4 * n + 4)
                nc.scalar.activation(xoT[:, :], ps[:, 6, :], ACT.Copy).then_inc(xoT_ready, 1)

            with act.Fori(0, B - 1) as b:
                for g in range(NG):
                    cross_group(b * NG + g, True)
            for g in range(NG):
                at = {NG - 2: (ROOTS_AT, lambda: ln_scalar(act, 0, NT - QT, 2 * B + 1)),
                      NG - 1: (EXP_AT, lambda: exp_logits(0, 0, NT - QT))}.get(g)
                cross_group((B - 1) * NG + g, g < NG - 1, at)

            ln_scalar(act, NT - QT, NT, 2 * B + 2)

            def silus(b, ms=range(FC)):
                for m in ms:
                    u = b * FC + m
                    act.wait_ge(h_filled, u + 1)
                    if u >= 2:
                        act.wait_ge(h_ready, u - 1)
                    nc.scalar.activation(gt[:, m % 2, :], ps[:, 2 * (m % 2), :], ACT.Silu).then_inc(silu_ready, 1)

            silus(0, range(2))
            exp_logits(1, NT - QT, NT)
            silus(0, range(2, FC))
            for b in range(1, SHARED_FIRST):
                silus(b)
            silus(SHARED_FIRST, range(SHARED_PIECES))
            act.wait_ge(h_ready, FC * SHARED_FIRST + SHARED_PIECES)

            def copy_rowsT(j, par):
                act.wait_ge(rowsT_filled, j + 1)
                nc.scalar.activation(xgT[:, par, :, :].rearrange("p c t -> p (c t)"), ps[:, 4, 0:D], ACT.Copy).then_inc(rowsT_ready, 1)

            def silu_rows(j, par):
                act.wait_ge(g13_filled, j + 1)
                nc.scalar.activation(gs[:, par, :], ps[:, 2 * par, :], ACT.Silu).then_inc(g_ready, 1)

            def copy_y(j, par, i):
                act.wait_ge(yrow_filled, j + 1)
                if not isinstance(i, int) or i > 0:
                    act.wait_ge(y_stored[par], 16 * i)
                nc.scalar.activation(yrow[:, par, :], ps[:, 6 + par, 0:D], ACT.Copy).then_inc(yrow_ready, 1)

            copy_rowsT(0, 0)
            copy_rowsT(1, 1)
            silu_rows(0, 0)
            slot_steps(act, lambda j, par, more, i: (copy_rowsT(j + 1, 1 - par) if more else None, silu_rows(j, par), copy_y(j - 1, 1 - par, i)))
            copy_y(MT - 1, 0, MT // 2)
            for b in range(SHARED_FIRST, B):
                silus(b, range(SHARED_PIECES if b == SHARED_FIRST else 0, FC))

        @block.vector
        def _(dve):
            def split_context(b):
                ms = [DC * b + c for c in range(DC)]
                for m in ms:
                    dve.wait_ge(ctxT_ready, m + 1)
                    if m >= PARTS:
                        dve.wait_ge(parts_stored[m % PARTS], 48 * (m // PARTS))
                    nc.vector.tensor_copy(part[:, m % PARTS, 0, :], ctxT[:, m, :]).then_inc(ctx_hi, 1)
                for m in ms:
                    dve.wait_ge(ctx_hi, m + 1)
                    nc.vector.tensor_tensor(rest[:, m % 2, :], ctxT[:, m, :], part[:, m % PARTS, 0, :], ALU.subtract).then_inc(ctx_rest1, 1)
                for m in ms:
                    dve.wait_ge(ctx_rest1, m + 1)
                    nc.vector.tensor_copy(part[:, m % PARTS, 1, :], rest[:, m % 2, :]).then_inc(ctx_mid, 1)
                for m in ms:
                    dve.wait_ge(ctx_mid, m + 1)
                    nc.vector.tensor_tensor(part[:, m % PARTS, 2, :], rest[:, m % 2, :], part[:, m % PARTS, 1, :],
                                            ALU.subtract).then_inc(ctx_parts_ready, 1)

            def rest_queries(b):
                for c in range(DC):
                    m = DC * b + c
                    dve.wait_ge(hi_ready, m + 1)
                    if m >= 2:
                        dve.wait_ge(parts_ready, m - 1)
                    nc.vector.scalar_tensor_tensor(rest[:, m % 2, :], ps[:, QBANK[m], :], XD ** -0.5, part[:, m % PARTS, 0, :],
                                                   ALU.mult, ALU.subtract).then_inc(rest1_ready, 1)

            def copy_k(n, b):
                dve.wait_ge(k_filled, n + 1)
                nc.vector.tensor_copy(kt[:, b % 2, W:], ps[:, BANK["k", 0], :]).then_inc(k_ready, 1)

            def copy_v(n, b):
                dve.wait_ge(v_filled, n + 1)
                nc.vector.tensor_copy(vv[:, b % 2, :, :].rearrange("p t n -> p (t n)"),
                                      ps[:, BANK["v", 0], :]).then_inc(v_ready, 1)

            def maxima(n, b, i):
                dve.wait_ge(scores_filled, QT * n + 2 * i + 2)
                s = ps[:, 2 * i:2 * i + 2, 0:2 * KW].rearrange("p t (h k) -> p t h k", h=2)
                m = mask[:, 0:2, :] if i == 0 else mask[:, 1:2, :].to_broadcast([P, 2, KW])
                nc.vector.tensor_tensor(s, s, m.unsqueeze(2).to_broadcast([P, 2, 2, KW]), ALU.add).then_inc(masked, 1)
                dve.wait_ge(masked, 2 * n + i + 1)
                nc.vector.tensor_reduce(nmax[:, b % 2, 4 * i:4 * i + 4].rearrange("p (t h) -> p t h", h=2), s, AXX, ALU.max,
                                        negate=True).then_inc(max_ready, 1)

            def inverse_sums(n, b, i):
                dve.wait_ge(exp_done, 2 * QT * n + 4 * i + 4)
                nc.vector.reciprocal(rinv[:, b % 2, 4 * i:4 * i + 4], rsum[:, b % 2, 4 * i:4 * i + 4]).then_inc(rinv_ready, 1)

            def copy_prT(n, t):
                src = ps[:, BANK["pT", t], :].rearrange("p (h k q) -> p h k q", h=2, k=2)
                dve.wait_ge(prT_filled, QT * n + t + 1)
                if t >= 1:
                    nc.vector.tensor_copy(prT[:, :, t - 1, P:KW], src[:, :, 0, 0:W]).then_inc(prT_ready, 1)
                nc.vector.tensor_copy(prT[:, :, t, 0:P], src[:, :, 1, :]).then_inc(prT_ready, 1)

            def add_y(n, b, i):
                tiles = xs[:, QT * b + 2 * i:QT * b + 2 * i + 2, :].rearrange("p t d -> p (t d)")
                dve.wait_ge(y_filled, 2 * n + i + 1)
                nc.vector.tensor_tensor(tiles, tiles, ps[:, BANK["y", i], :], ALU.add).then_inc(x1_ready, 1)

            for b in range(B):
                dve.wait_ge(x_loaded[b], 16)
                ln_stats(dve, 0, QT * b, QT * (b + 1))
                if b >= 1:
                    ln_rows(dve, 0, QT * (b - 1), QT * b, b)
            dve.wait_ge(zeros_ready, 4)
            dve.wait_ge(masks_ready, 2)
            copy_k(0, 0)
            copy_v(0, 0)
            ln_rows(dve, 0, NT - QT, NT, B)

            def pair_step(hp, b, prior, more, first, last):
                n, pb, nb = hp * B + b, (b - 1) % B, (b + 1) % B
                for i in range(2):
                    if prior:
                        for t in range(2 * i, 2 * i + 2):
                            copy_prT(n - 1, t)
                    maxima(n, b, i)
                if last and b >= 2:
                    ln_stats(dve, 1, QT * (b - 2), QT * (b - 1))
                if more:
                    copy_k(n + 1, nb)
                inverse_sums(n, b, 0)
                if prior:
                    add_y(n - 1, pb, 0)
                if more:
                    copy_v(n + 1, nb)
                inverse_sums(n, b, 1)
                if prior:
                    add_y(n - 1, pb, 1)
                if first:
                    split_context(b)
                if last and b >= 2:
                    ln_rows(dve, 1, QT * (b - 2), QT * (b - 1), B + b - 1)

            def pair_finish(n, b):
                rest_queries(0)
                for t in range(QT):
                    copy_prT(n, t)
                ln_stats(dve, 1, 2 * QT, 3 * QT)
                rest_queries(1)
                ln_rows(dve, 1, 2 * QT, 3 * QT, B + 3)
                for i in range(2):
                    add_y(n, b, i)
                dve.wait_ge(x1_ready, 2 * HP * B)
                ln_stats(dve, 1, 3 * QT, NT)
                rest_queries(2)
                ln_rows(dve, 1, 3 * QT, NT, B + 4)
                rest_queries(3)

            pair_steps(dve, pair_step, pair_finish)

            def cross_max(n, par, u):
                h, q2 = u // 2, u % 2
                dve.wait_ge(xs_filled, 8 * n + u + 1)
                nc.vector.tensor_reduce(xnm[:, par, h, 2 * q2:2 * q2 + 2], ps[:, 2 * (u % 2):2 * (u % 2) + 2, :], AXX,
                                        ALU.max, negate=True).then_inc(nmax_ready, 1)
                if u == 7:
                    cross_split_max(n, par)

            def cross_split_max(n, par):
                dve.wait_ge(nmax_ready, 8 * n + 8)
                nc.vector.tensor_copy(xm2[:, par, 0, :, :], xnm[:, par, :, :]).then_inc(part1_ready, 1)
                dve.wait_ge(part1_ready, n + 1)
                nc.vector.tensor_tensor(xm2[:, par, 1, :, :], xnm[:, par, :, :], xm2[:, par, 0, :, :],
                                        ALU.subtract).then_inc(m2_ready, 1)

            def cross_add(n, b, g):
                sums = ps[:, 7, :].rearrange("p (t h d) -> p t h d", t=QT, h=HG)
                dve.wait_ge(xoN_filled, n + 1)
                nc.vector.reciprocal(xr[:, :, :], sums[:, :, :, XD]).then_inc(xr_ready, 1)
                dve.wait_ge(xr_ready, n + 1)
                nc.vector.tensor_tensor(xo[:, :, :, :], sums[:, :, :, 0:XD],
                                        xr[:, :, :].unsqueeze(3).to_broadcast([P, QT, HG, XD]), ALU.mult).then_inc(xo_ready, 1)
                dve.wait_ge(xo_ready, n + 1)
                part_x = xs[:, bass.ds(b * QT, QT), g * HG * XD:(g + 1) * HG * XD]
                nc.vector.tensor_tensor(part_x, part_x, xo[:, :, :, :].rearrange("p t h d -> p t (h d)"),
                                        ALU.add).then_inc(x2_ready, 1)

            for w in range(AHEAD + 1):
                cross_max(w // 8, w // 8 % 2, w % 8)

            def cross_group(n, b, g, units=8):
                for i in range(units):
                    w = AHEAD + 1 + i
                    cross_max(n + w // 8, (g + w // 8) % 2, w % 8)
                cross_add(n, b, g)

            def units_left(g):
                return max(0, min(8, UNITS - AHEAD - 1 - 8 * ((B - 1) * NG + g)))

            with dve.Fori(0, B - 1) as b:
                for g in range(NG):
                    cross_group(b * NG + g, b, g)
            def copy_xn3T(m):
                dve.wait_ge(turned, 2 * B * DC + m + 1)
                nc.vector.tensor_copy(xnT[:, m % DC, (m // DC) * S:(m // DC + 1) * S], ps[:, XBANK[m], :]).then_inc(xn3T_ready, 1)

            steps = [0]

            def then(op):
                steps[0] += 1
                op.then_inc(route, 1)
                dve.wait_ge(route, steps[0])

            def choose(k, t0, t1):
                nt = t1 - t0
                dve.wait_ge(logits_filled, k + 1)
                logits = ps[:, (3, 7)[k], 0:nt * NE].rearrange("p (t e) -> p t e", e=NE)
                then(nc.vector.tensor_reduce(lmax[:, t0:t1], logits, AXX, ALU.max))
                nc.vector.tensor_tensor(lg[:, t0:t1, :], logits, lmax[:, t0:t1].unsqueeze(2).to_broadcast([P, nt, NE]),
                                        ALU.subtract).then_inc(e_ready, 1)
                dve.wait_ge(exp_e_ready, k + 1)
                for t in range(t0, t1):
                    last = nc.vector.max(top[:, t, :], lg[:, t, :])
                then(last)
                for t in range(t0, t1):
                    last = nc.vector.max_index(tix[:, t, :], top[:, t, :], lg[:, t, :])
                then(last)
                then(nc.vector.tensor_copy(tixf[:, t0:t1, :], tix[:, t0:t1, 0:TOP]))
                for i in range(TOP):
                    last = nc.vector.tensor_tensor(hot[:, i, t0:t1, :], iota8[:, :].unsqueeze(1).to_broadcast([P, nt, NE]),
                                                   tixf[:, t0:t1, i:i + 1].to_broadcast([P, nt, NE]), ALU.is_equal)
                then(last)
                nc.vector.tensor_tensor(sel[:, t0:t1, :], hot[:, 0, t0:t1, :], hot[:, 1, t0:t1, :], ALU.add).then_inc(sel_ready, 1)

            dve.wait_ge(route_consts_ready, 6)
            for g in range(NG - 1):
                if g == NG - 2:
                    ln_rows(dve, 2, 0, NT - QT, 2 * B + 1)
                cross_group((B - 1) * NG + g, B - 1, g, units_left(g))
                if g == NG - 3:
                    dve.wait_ge(x2_ready, (B - 1) * NG)
                    ln_stats(dve, 2, 0, NT - QT)
            for m in range(DC * (B - 1)):
                copy_xn3T(m)
            choose(0, 0, NT - QT)
            cross_group(B * NG - 1, B - 1, NG - 1, 0)

            dve.wait_ge(x2_ready, B * NG)
            ln_stats(dve, 2, NT - QT, NT)
            ln_rows(dve, 2, NT - QT, NT, 2 * B + 2)
            for m in range(DC * (B - 1), DC * B):
                copy_xn3T(m)

            def hidden(b, ms=range(FC)):
                for m in ms:
                    dve.wait_ge(silu_ready, b * FC + m + 1)
                    nc.vector.tensor_tensor(ht[:, b % 2, m, :], gt[:, m % 2, :], ps[:, 2 * (m % 2) + 1, :],
                                            ALU.mult).then_inc(h_ready, 1)

            hidden(0, range(2))
            choose(1, NT - QT, NT)
            hidden(0, range(2, 3))
            dve.wait_ge(counts_filled, 1)
            in_tile = ps[:, 6, 0:NT * NE].rearrange("p (t e) -> p t e", e=NE)
            totals = ps[:, 6, NT * NE:2 * NT * NE].rearrange("p (t e) -> p t e", e=NE)
            then(nc.vector.tensor_copy(run[:, 0, 8:, :], totals))
            for k, d in enumerate((1, 2, 4, 8)):
                then(nc.vector.tensor_tensor(run[:, (k + 1) % 2, 8:, :], run[:, k % 2, 8:, :], run[:, k % 2, 8 - d:8 + NT - d, :], ALU.add))
            then(nc.vector.tensor_scalar(tiles_f[:, :], run[:, 0, 7 + NT, :], float(P - 1), None, ALU.add))
            then(nc.vector.tensor_copy(tiles_i[:, :], tiles_f[:, :]))
            then(nc.vector.tensor_scalar(tiles_i[:, :], tiles_i[:, :], 7, None, ALU.logical_shift_right))
            then(nc.vector.tensor_copy(ends[:, 0, 4:], tiles_i[:, :]))
            for k, d in enumerate((1, 2, 4)):
                then(nc.vector.tensor_tensor(ends[:, (k + 1) % 2, 4:], ends[:, k % 2, 4:], ends[:, k % 2, 4 - d:4 + NE - d], ALU.add))
            then(nc.vector.tensor_tensor(slot_e[:, :, :], in_tile, run[:, 0, 7:7 + NT, :], ALU.add))
            then(nc.vector.tensor_scalar(tiles_f[:, :], ends[:, 1, 3:3 + NE], float(P), None, ALU.mult))
            then(nc.vector.tensor_tensor(slot_e[:, :, :], slot_e[:, :, :], tiles_f[:, :].unsqueeze(1).to_broadcast([P, NT, NE]), ALU.add))
            for i in range(TOP):
                last = nc.vector.tensor_tensor(hot[:, i, :, :], hot[:, i, :, :], slot_e[:, :, :], ALU.mult)
            then(last)
            then(nc.vector.tensor_reduce(slot_f[:, :, :], hot[:, :, :, :], AXX, ALU.add))
            nc.vector.tensor_copy(slot[:, :, :], slot_f[:, :, :]).then_inc(slots_ready, 1)
            then(nc.vector.tensor_tensor(owner_e[:, :, :], iota_mt[:, :].unsqueeze(2).to_broadcast([1, MT, NE - 1]),
                                         ends[0:1, 1, 4:3 + NE].unsqueeze(1).to_broadcast([1, MT, NE - 1]), ALU.is_ge))
            then(nc.vector.tensor_reduce(owner_f[:, :], owner_e[:, :, :], AXX, ALU.add))
            nc.vector.tensor_copy(owner[:, :], owner_f[:, :]).then_inc(owner_ready, 1)
            hidden(0, range(3, FC))
            then(nc.vector.tensor_tensor(gsum[:, :], top[:, :, 0], top[:, :, 1], ALU.add))
            then(nc.vector.reciprocal(gsum[:, :], gsum[:, :]))
            then(nc.vector.tensor_tensor(gate[:, :, :], top[:, :, 0:TOP], gsum[:, :].unsqueeze(2).to_broadcast([P, NT, TOP]), ALU.mult))

            def add_shared(b):
                for i in range(2):
                    dve.wait_ge(e_filled, 2 * b + i + 1)
                    two = xs[:, QT * b + 2 * i:QT * b + 2 * i + 2, :].rearrange("p t d -> p (t d)")
                    nc.vector.tensor_tensor(two, two, ps[:, 4 + 2 * (b % 2) + i, :], ALU.add).then_inc(e_added, 1)

            for b in range(SHARED_FIRST):
                if b:
                    hidden(b)
                add_shared(b)

            hidden(SHARED_FIRST, range(SHARED_PIECES))

            def hid_rows(j, par):
                dve.wait_ge(g_ready, j + 1)
                nc.vector.tensor_tensor(hid[:, par, :], gs[:, par, :], ps[:, 2 * par + 1, :], ALU.mult).then_inc(hid_ready, 1)

            def copy_hidT(j, par):
                dve.wait_ge(hidT_filled, j + 1)
                nc.vector.tensor_copy(hidT[:, par, :, :].rearrange("p m t -> p (m t)"), ps[:, 5, :]).then_inc(hidT_ready, 1)

            hid_rows(0, 0)
            slot_steps(dve, lambda j, par, more, i: (copy_hidT(j - 1, 1 - par), hid_rows(j, par)))
            copy_hidT(MT - 1, (MT - 1) % 2)

            def combine(b):
                dve.wait_ge(e_added, 2 * b + 2)
                for t in range(QT * b, QT * (b + 1)):
                    dve.wait_ge(y_gathered[t], 16 * TOP)
                    nc.vector.scalar_tensor_tensor(xs[:, t, :], yg[:, TOP * t, :], gate[:, t, 0:1], xs[:, t, :],
                                                   ALU.mult, ALU.add).then_inc(combined0, 1)
                for t in range(QT * b, QT * (b + 1)):
                    dve.wait_ge(combined0, t + 1)
                    nc.vector.scalar_tensor_tensor(xs[:, t, :], yg[:, TOP * t + 1, :], gate[:, t, 1:2], xs[:, t, :],
                                                   ALU.mult, ALU.add).then_inc(combined, 1)

            for b in range(SHARED_FIRST, B):
                hidden(b, range(SHARED_PIECES if b == SHARED_FIRST else 0, FC))
                if b < B - 1:
                    combine(b - SHARED_FIRST)
                    add_shared(b)
            for b in range(B - 1 - SHARED_FIRST, B - 1):
                combine(b)
            add_shared(B - 1)
            combine(B - 1)

        @block.tensor
        def _(pe):
            def turn_rows1(b):
                for c in range(DC):
                    n = DC * b + c
                    pe.wait_ge(xn_ready, QT * (b + 1))
                    if n >= 4:
                        pe.wait_ge(xnT_ready, n - 3)
                    turn(pe, xn, b, c, n % 4, turned)

            def turn_context(m):
                if m == 0:
                    pe.wait_ge(c_loaded, 16)
                else:
                    pe.wait_ge(ctxT_ready, m)
                turn(pe, cs, m // DC, m % DC, 6, ctx_turned)

            def turn_queries(b):
                pe.wait_ge(xn_ready, NT + QT * (b + 1))
                for c in range(DC):
                    turn(pe, xn, b, c, QBANK[DC * b + c], turned)

            left = {}

            def use_bank(use, n, tells):
                bank = BANK[use]
                if bank in left:
                    s, step, count, m = left[bank]
                    pe.wait_ge(s, (n + (m - now[0])) * step + count)
                s, step, count, ahead = tells
                left[bank] = (s, step, count, now[0] + ahead)
                return ps[:, bank, :]

            now = [0]

            def project_qk(s, b, n):
                name, filled, ready, each = (("q", q_filled, q_ready, 2), ("k", k_filled, k_ready, 1))[s]
                o = use_bank((name, 0), n, (ready, each, each, 1))
                for c in range(DC):
                    mm = nc.tensor.matmul(o, wqkv[:, c, s, :], xnT[:, c, b * S:(b + 1) * S], start=(c == 0), stop=(c == DC - 1))
                mm.then_inc(filled, 1)

            def project_v(b, n):
                o = use_bank(("v", 0), n, (v_ready, 1, 1, 1))
                for t in range(QT):
                    for c in range(DC):
                        k0 = b * S + t * P
                        mm = nc.tensor.matmul(o[:, t * P:(t + 1) * P], xnT[:, c, k0:k0 + P], wqkv[:, c, 2, :],
                                              start=(c == 0), stop=(c == DC - 1))
                mm.then_inc(v_filled, 1)

            def scores(n, b, prior, ts):
                pe.wait_ge(q_ready, 2 * n + 2)
                pe.wait_ge(k_ready, n + 1)
                for t in ts:
                    if prior:
                        pe.wait_ge(exp_done, 2 * QT * (n - 1) + 2 * t + 2)
                    for h in range(2):
                        o = ps[:, t, h * KW:(h + 1) * KW]
                        q = (qa, qb)[h][:, b % 2, t * P:(t + 1) * P]
                        mm = nc.tensor.matmul(o, q, kt[:, b % 2, t * P:t * P + KW], start=True, stop=True)
                    mm.then_inc(scores_filled, 1)

            def turn_probs(n, b, t):
                pe.wait_ge(probs_ready, QT * (n - 1) + t + 1)
                o = use_bank(("pT", t), n, (prT_ready, 7, 2 * t + 1, -1))
                for h in range(2):
                    for k in ((1,) if t == 0 else (0, 1)):
                        mm = nc.tensor.transpose(o[:, (2 * h + k) * P:(2 * h + k + 1) * P], pr[:, b % 2, t, h, k * P:(k + 1) * P], ident[:])
                mm.then_inc(prT_filled, 1)

            def attend(n, b):
                pe.wait_ge(prT_ready, 7 * n)
                pe.wait_ge(v_ready, n)
                for t in range(QT):
                    w = KW if t < QT - 1 else P
                    for h in range(2):
                        mm = nc.tensor.matmul(ps[h * DH:(h + 1) * DH, 6, t * P:t * P + w], vv[:, b % 2, t, h * DH:(h + 1) * DH],
                                              prT[:, h, t, 0:w], start=(t == 0), stop=(t == QT - 1), skip_group_check=True)
                mm.then_inc(oT_filled, 1)

            def project_out(n, b, i):
                pe.wait_ge(oT_ready, n)
                o = use_bank(("y", i), n, (x1_ready, 2, i + 1, -1))
                for j in range(2):
                    t = 2 * i + j
                    mm = nc.tensor.matmul(o[:, j * D:(j + 1) * D], oT[:, t * P:(t + 1) * P], wo[:, :], start=True, stop=True)
                mm.then_inc(y_filled, 1)

            pe.wait_ge(ident_ready, 1)
            turn_rows1(0)
            turn_rows1(1)
            pe.wait_ge(wqkv_loaded, 32)
            pe.wait_ge(xnT_ready, DC)
            now[0] = -1
            for s in range(2):
                project_qk(s, 0, -1)
            project_v(0, -1)
            turn_rows1(2)
            turn_rows1(3)
            pe.wait_ge(xnT_ready, B * DC)
            pe.wait_ge(zeros_ready, 4)

            def pair_step(hp, b, prior, more, first, last):
                n, pb, nb = hp * B + b, (b - 1) % B, (b + 1) % B
                now[0] += 1
                scores(n, b, prior, range(2))
                if prior:
                    for t in range(QT - 1):
                        turn_probs(n, pb, t)
                scores(n, b, prior, range(2, QT))
                if prior:
                    turn_probs(n, pb, QT - 1)
                if first:
                    if prior:
                        pe.wait_ge(oT_ready, n - 1)
                    turn_context(DC * b)
                if more:
                    if nb == 0:
                        pe.wait_ge(wqkv_loaded, 32 * (hp + 1) + 32)
                    project_qk(0, nb, n)
                if prior:
                    if first:
                        pe.wait_ge(ctxT_ready, DC * b + 1)
                    attend(n, pb)
                if more:
                    project_qk(1, nb, n)
                if prior:
                    if pb == 0:
                        pe.wait_ge(wo_loaded, 16 * hp + 16)
                    project_out(n, pb, 0)
                if more:
                    project_v(nb, n)
                if prior:
                    project_out(n, pb, 1)
                if first:
                    turn_context(DC * b + 1)
                    if b == B - 1:
                        pe.wait_ge(ctxT_ready, B * DC)

            def pair_finish(n, b):
                now[0] += 1
                pe.wait_ge(exp_done, 2 * QT * (n + 1))
                turn_queries(0)
                for t in range(QT):
                    turn_probs(n + 1, b, t)
                turn_queries(1)
                attend(n + 1, b)
                for i in range(2):
                    project_out(n + 1, b, i)
                turn_queries(2)
                pe.wait_ge(x1_ready, 2 * (n + 1))
                turn_queries(3)

            pair_steps(pe, pair_step, pair_finish)

            def cross_scores(n, g, u):
                h, q2 = u // 2, u % 2
                hh = HG * g + h
                if u >= 2 or not isinstance(n, int) or n > 0:
                    pe.wait_ge(nmax_ready, 8 * n + u - 1)
                for j in range(2):
                    mm = nc.tensor.matmul(ps[:, 2 * (u % 2) + j, :], qp[0:XS, hh, (2 * q2 + j) * P:(2 * q2 + j + 1) * P],
                                          kp[0:XS, hh, :], start=True, stop=True)
                mm.then_inc(xs_filled, 1)

            def turn_max(n, par, left=0):
                pe.wait_ge(m2_ready, n + 1)
                if left:
                    pe.wait_ge(x2_ready, left)
                for t in range(QT):
                    o = ps[0:2 * HG, 7, t * P // 2:(t + 1) * P // 2].bitcast(BF16)
                    src = xm2[:, par, :, :, t].rearrange("p i h -> p (i h)")
                    mm = nc.tensor.transpose(o, src, ident_b[:])
                mm.then_inc(m2T_filled, 1)

            def cross_exp_scores(n, g, u):
                k, h = u // HG, u % HG
                if not isinstance(n, int) or n > 0 or u >= 2:
                    pe.wait_ge(ex_ready, 16 * n + u - 1)
                mm = nc.tensor.matmul(ps[:, 4 + u % 2, :], kp[0:XS + 2, HG * g + h, k * P:(k + 1) * P], qp[0:XS + 2, HG * g + h, :],
                                      start=True, stop=True)
                mm.then_inc(st_filled, 1)

            def cross_values(n, g, k):
                pe.wait_ge(ex_ready, 16 * n + 4 * k + 4)
                for h in range(HG):
                    mm = nc.tensor.matmul(ps[32 * h:32 * h + 32, 6, :], vp[:, k, HG * g + h, :], ex[:, k % 2, h, :],
                                          start=(k == 0), stop=(k == QT - 1), skip_group_check=True)
                mm.then_inc(pv_done, 1)

            pe.wait_ge(rest1_ready, 2 * DC)
            pe.wait_ge(cross_consts_ready, 2)
            def scores_unit(n, b, g, w):
                m, u = w // 8, w % 8
                if u == 0:
                    pe.wait_ge(split_loaded[(g + m) % NG], 16 * 9 * (b + 1 + (g + m) // NG))
                cross_scores(n + m, (g + m) % NG, u)

            for w in range(AHEAD):
                scores_unit(0, 0, 0, w)
                if w == 8:
                    pe.wait_ge(rest1_ready, B * DC)
                    turn_max(0, 0)
            pe.wait_ge(m_loaded, 32)
            for u in range(2):
                cross_exp_scores(0, 0, u)

            def cross_group(n, b, g, units, more, beside=None):
                for i in range(8):
                    if i < 7:
                        even, unit = i % 2 == 0, i < units
                        if even and unit:
                            scores_unit(n, b, g, AHEAD + i)
                        cross_exp_scores(n, g, 2 * i + 2)
                        if not even and unit:
                            scores_unit(n, b, g, AHEAD + i)
                        if i == 3 and more:
                            turn_max(n + 1, (g + 1) % 2, left=0 if units == 8 else n)
                        if i in (2, 4):
                            if g == 0 and i == 2:
                                pe.wait_ge(vp_ready, QT * (b + 1))
                            cross_values(n, g, i // 2 - 1)
                        cross_exp_scores(n, g, 2 * i + 3)
                        if i == 6:
                            cross_values(n, g, 2)
                    if beside:
                        beside(i)
                if more:
                    pe.wait_ge(m_loaded, 32 * (n + 2))
                    cross_exp_scores(n + 1, (g + 1) % NG, 0)
                cross_values(n, g, 3)
                if units == 8:
                    scores_unit(n, b, g, AHEAD + 7)
                if more:
                    cross_exp_scores(n + 1, (g + 1) % NG, 1)
                pe.wait_ge(xoT_ready, n + 1)
                pe.wait_ge(m2T_ready, n + 2 if more else n + 1)
                if units < 8:
                    pe.wait_ge(x2_ready, n)
                for t in range(QT):
                    mm = nc.tensor.transpose(ps[:, 7, t * P:(t + 1) * P], xoT[:, t * P:(t + 1) * P], ident[:])
                mm.then_inc(xoN_filled, 1)

            with pe.Fori(0, B - 1) as b:
                for g in range(NG):
                    cross_group(b * NG + g, b, g, 8, True)

            def turn_rows3(m):
                if 3 <= m < 6:
                    pe.wait_ge(xn3T_ready, m - 2)
                turn(pe, xn, m // DC, m % DC, XBANK[m], turned)

            def logits(k, t0, t1):
                for t in range(t0, t1):
                    for c in range(DC):
                        o = ps[:, (3, 7)[k], (t - t0) * NE:(t - t0 + 1) * NE]
                        mm = nc.tensor.matmul(o, xnT[:, c, t * P:(t + 1) * P], wr[:, c, :], start=(c == 0), stop=(c == DC - 1))
                mm.then_inc(logits_filled, 1)

            def rows_beside(i):
                if i == 1:
                    pe.wait_ge(nmax_ready, UNITS)
                if 1 <= i <= 6:
                    pe.wait_ge(xn_ready, 2 * NT + QT * ((i - 1) // DC + 1))
                    turn_rows3(i - 1)
                if i == 7:
                    pe.wait_ge(wr_loaded, 16)
                    pe.wait_ge(xn3T_ready, DC * (B - 1))
                    logits(0, 0, NT - QT)

            for g in range(NG):
                units = max(0, min(8, UNITS - AHEAD - 8 * ((B - 1) * NG + g)))
                cross_group((B - 1) * NG + g, B - 1, g, units, g < NG - 1, rows_beside if g == NG - 1 else None)

            def shared_hidden(b, ms=range(FC)):
                for m in ms:
                    u = b * FC + m
                    if u >= 2:
                        pe.wait_ge(h_ready, u - 1)
                    for w, bank in ((wa, 2 * (m % 2)), (wb, 2 * (m % 2) + 1)):
                        for c in range(DC):
                            mm = nc.tensor.matmul(ps[:, bank, :], w[:, c, m * P:(m + 1) * P], xnT[:, c, b * S:(b + 1) * S],
                                                  start=(c == 0), stop=(c == DC - 1))
                    mm.then_inc(h_filled, 1)

            pe.wait_ge(shared_loaded, 48)
            pe.wait_ge(xn3T_ready, DC * (B - 1))
            pe.wait_ge(e_ready, 1)
            shared_hidden(0, range(2))
            pe.wait_ge(xn_ready, 3 * NT)
            pe.wait_ge(ex_ready, 16 * B * NG)
            for m in range(DC * (B - 1), DC * B):
                turn_rows3(m)
            pe.wait_ge(xn3T_ready, B * DC)
            pe.wait_ge(x2_ready, B * NG)
            logits(1, NT - QT, NT)

            def shared_out(b):
                pe.wait_ge(h_ready, (b + 1) * FC)
                if b >= 2:
                    pe.wait_ge(e_added, 2 * b - 2)
                for i in range(2):
                    for j in range(2):
                        t = 2 * i + j
                        for m in range(FC):
                            mm = nc.tensor.matmul(ps[:, 4 + 2 * (b % 2) + i, j * D:(j + 1) * D], ht[:, b % 2, m, t * P:(t + 1) * P],
                                                  wc[:, m, :], start=(m == 0), stop=(m == FC - 1))
                    mm.then_inc(e_filled, 1)

            for b in range(SHARED_FIRST):
                if b == 0:
                    shared_hidden(0, range(2, 3))
                    pe.wait_ge(sel_ready, 2)
                    pe.wait_ge(route_consts_ready, 6)
                    chosen = sel[:, :, :].rearrange("p t e -> p (t e)")
                    nc.tensor.matmul(ps[:, 6, 0:P], before[:], chosen, start=True, stop=True)
                    nc.tensor.matmul(ps[:, 6, P:2 * P], ones[:], chosen, start=True, stop=True).then_inc(counts_filled, 1)
                    shared_hidden(0, range(3, FC))
                    shared_hidden(1, range(1))
                else:
                    shared_hidden(b, range(1 if b == 1 else 0, FC))
                if b == 1:
                    pe.wait_ge(slots_ready, 1)
                shared_out(b)

            def turn_rows(j, par, loads):
                pe.wait_ge(rows_loaded[par], 16 * loads)
                for c in range(DC):
                    mm = nc.tensor.transpose(ps[:, 4, c * P:(c + 1) * P], xg[:, par, c * P:(c + 1) * P], ident[:])
                mm.then_inc(rowsT_filled, 1)

            def rows_hidden(j, par):
                e = pe.value_load(owner[0:1, bass.ds(j, 1)], min_val=0, max_val=NE - 1)
                pe.wait_ge(rowsT_ready, j + 1)
                for w, bank in ((w1s, 2 * par), (w3s, 2 * par + 1)):
                    we = w[:, bass.ds(e, 1), :].rearrange("p e (c f) -> p (e c) f", c=DC)
                    for c in range(DC):
                        mm = nc.tensor.matmul(ps[:, bank, :], xgT[:, par, c, :], we[:, c, :], start=(c == 0), stop=(c == DC - 1))
                mm.then_inc(g13_filled, 1)

            def turn_hid(j, par):
                pe.wait_ge(hid_ready, j + 1)
                for m in range(FC):
                    mm = nc.tensor.transpose(ps[:, 5, m * P:(m + 1) * P], hid[:, par, m * P:(m + 1) * P], ident[:])
                mm.then_inc(hidT_filled, 1)

            def rows_out(j, par):
                e = pe.value_load(owner[0:1, bass.ds(j, 1)], min_val=0, max_val=NE - 1)
                pe.wait_ge(hidT_ready, j + 1)
                we = w2s[:, bass.ds(e, 1), :].rearrange("p e (m d) -> p (e m) d", m=FC)
                for m in range(FC):
                    mm = nc.tensor.matmul(ps[:, 6 + par, 0:D], hidT[:, par, m, :], we[:, m, :], start=(m == 0), stop=(m == FC - 1))
                mm.then_inc(yrow_filled, 1)

            shared_hidden(SHARED_FIRST, range(SHARED_PIECES))
            pe.wait_ge(owner_ready, 1)
            pe.wait_ge(w13_loaded, 16 * 2 * NE)
            pe.wait_ge(w2_loaded, 16 * NE)
            pe.wait_ge(e_added, 2 * SHARED_FIRST)
            pe.wait_ge(h_ready, FC * SHARED_FIRST + SHARED_PIECES)
            turn_rows(0, 0, 1)
            pe.wait_ge(rowsT_ready, 1)
            turn_rows(1, 1, 1)
            rows_hidden(0, 0)

            def slot_step(j, par, more, i):
                if more:
                    pe.wait_ge(rowsT_ready, j + 1)
                    turn_rows(j + 1, 1 - par, i + 2)
                turn_hid(j - 1, 1 - par)
                rows_hidden(j, par)
                rows_out(j - 1, 1 - par)

            slot_steps(pe, slot_step)
            turn_hid(MT - 1, (MT - 1) % 2)
            rows_out(MT - 1, (MT - 1) % 2)
            pe.wait_ge(yrow_ready, MT)
            for b in range(SHARED_FIRST, B):
                shared_hidden(b, range(SHARED_PIECES if b == SHARED_FIRST else 0, FC))
                shared_out(b)


_INS = ["x", "ctx_1024", "L0_attn_w_qkv", "L0_attn_w_out", "L0_ffn_w_router", "L0_ffn_w1", "L0_ffn_w3", "L0_ffn_w2",
        "L0_ffn_sw1", "L0_ffn_sw3", "L0_ffn_sw2"]
_OUTS = [((4, 512, 256), "float32")]


def kernel(**inputs):
    import numpy as _np
    import concourse.bacc as _bacc
    from concourse import mybir as _mybir
    from concourse.bass_utils import run_bass_kernel_spmd as _run

    nc = _bacc.Bacc("TRN2", target_bir_lowering=False, num_devices=1)
    arrays, args = {}, []
    for name in _INS:
        a = _np.ascontiguousarray(inputs[name])
        arrays[f"in_{name}_dram"] = a
        args.append(nc.dram_tensor(f"in_{name}_dram", a.shape, _mybir.dt.from_np(a.dtype), kind="ExternalInput").ap())
    for i, (shape, dtype) in enumerate(_OUTS):
        dt = _mybir.dt.from_np(_np.dtype(dtype))
        args.append(nc.dram_tensor(f"out_{i}_dram", shape, dt, kind="ExternalOutput").ap())
    decoder_layer(nc, *args)
    r = _run(nc, [arrays], core_ids=[0])
    return r.results[0]["out_0_dram"]
```
